# Optimizing a Trainium2 kernel written in Bass

```python
import numpy as np
import jax
import jax.numpy as jnp

def _softmax(x, axis=-1):
    return jax.nn.softmax(x, axis=axis)

def _gelu(x):
    return jax.nn.gelu(x, approximate=True)

def _silu(x):
    return jax.nn.silu(x)

def _sigmoid(x):
    return jax.nn.sigmoid(x)

def _layernorm(x, axis=-1, eps=1e-05):
    m = jnp.mean(x, axis=axis, keepdims=True)
    v = jnp.var(x, axis=axis, keepdims=True)
    return (x - m) / jnp.sqrt(v + eps)

def _scatter_add(tgt, idx, src, axis=0):
    return tgt.at[idx].add(src)

def _segment_sum(src, seg, n):
    return jax.ops.segment_sum(src, seg, n)
kernel_name = 'mk_vit_tower_d1_tok_img768_r4_9d70ae'

def setup_inputs(seed: int=0):
    np.random.seed(seed)
    _w = jnp.asarray

    def _rec_inputs():
        import jax
        import jax.numpy as jnp
        _rk = jax.random.key(seed)
        x = -0.000147625 + 0.999875 * jax.random.normal(jax.random.fold_in(_rk, 1), (64, 12, 224, 224), jnp.float32)
        return x
    x = _rec_inputs()

    def _L0_tok_setup():
        import jax, jax.numpy as jnp
        import numpy as np
        IMG = 224
        PATCH = 16
        EMBED = 192
        C = 12
        B = 64
        key = jax.random.key(seed)
        k1, k2 = jax.random.split(key)
        x = jax.random.normal(k1, (B, C, IMG, IMG), dtype=jnp.float32)
        channel_weights = jax.random.normal(k2, (C, EMBED), dtype=jnp.float32)
        return {'x': x, 'channel_weights': channel_weights}
    _L0_tok_all = _L0_tok_setup()
    _L0_tok_in = {k: v for k, v in _L0_tok_all.items() if k in ('channel_weights',)}
    del _L0_tok_all

    def _L0_attn_setup():
        import jax, jax.numpy as jnp
        import numpy as np
        B, N, C = (8, 256, 192)
        H = 12
        D = C // H
        SCALE = D ** (-0.5)
        EPS = 1e-05

        def _layer_norm(x):
            mean = x.mean(-1, keepdims=True)
            var = ((x - mean) ** 2).mean(-1, keepdims=True)
            return (x - mean) / jnp.sqrt(var + EPS)
        key = jax.random.key(seed)
        k1, k2, k3 = jax.random.split(key, 3)
        x = jax.random.normal(k1, (B, N, C), dtype=jnp.float32)
        qkv_weight = jax.random.normal(k2, (3 * C, C), dtype=jnp.float32) * C ** (-0.5)
        proj_weight = jax.random.normal(k3, (C, C), dtype=jnp.float32) * C ** (-0.5)
        return {'x': x, 'qkv_weight': qkv_weight, 'proj_weight': proj_weight}
    _L0_attn_all = _L0_attn_setup()
    _L0_attn_in = {k: v for k, v in _L0_attn_all.items() if k in ('qkv_weight', 'proj_weight')}
    del _L0_attn_all

    def _L0_ffn_setup():
        import jax, jax.numpy as jnp
        import numpy as np
        B_SZ, S, D = (8, 128, 192)
        H = 12
        N_EXP = 8
        RANK = 16
        ALPHA = 32
        TOP_K = 2
        key = jax.random.key(seed)
        ks = jax.random.split(key, 9)
        x = jax.random.normal(ks[0], (B_SZ, S, D), jnp.float32)
        W_qkv = jax.random.normal(ks[1], (3 * D, D), jnp.float32) * 0.02
        b_qkv = jnp.zeros((3 * D,), jnp.float32)
        W_gate = jax.random.normal(ks[2], (N_EXP, D), jnp.float32) * 0.02
        b_gate = jnp.zeros((N_EXP,), jnp.float32)
        A = jax.random.normal(ks[3], (N_EXP, RANK, D), jnp.float32) * 0.02
        B_lora = jax.random.normal(ks[4], (N_EXP, 3 * D, RANK), jnp.float32) * 0.02
        W_proj = jax.random.normal(ks[5], (D, D), jnp.float32) * 0.02
        b_proj = jnp.zeros((D,), jnp.float32)
        return {'x': x, 'W_qkv': W_qkv, 'b_qkv': b_qkv, 'W_gate': W_gate, 'b_gate': b_gate, 'A': A, 'B_lora': B_lora, 'W_proj': W_proj, 'b_proj': b_proj}
    _L0_ffn_all = _L0_ffn_setup()
    _L0_ffn_in = {k: v for k, v in _L0_ffn_all.items() if k in ('W_qkv', 'b_qkv', 'W_gate', 'b_gate', 'A', 'B_lora', 'W_proj', 'b_proj')}
    del _L0_ffn_all
    return {'x': x, 'L0_tok_channel_weights': _L0_tok_in['channel_weights'], 'L0_attn_qkv_weight': _L0_attn_in['qkv_weight'], 'L0_attn_proj_weight': _L0_attn_in['proj_weight'], 'L0_ffn_W_qkv': _L0_ffn_in['W_qkv'], 'L0_ffn_b_qkv': _L0_ffn_in['b_qkv'], 'L0_ffn_W_gate': _L0_ffn_in['W_gate'], 'L0_ffn_b_gate': _L0_ffn_in['b_gate'], 'L0_ffn_A': _L0_ffn_in['A'], 'L0_ffn_B_lora': _L0_ffn_in['B_lora'], 'L0_ffn_W_proj': _L0_ffn_in['W_proj'], 'L0_ffn_b_proj': _L0_ffn_in['b_proj']}

def reference(x, L0_tok_channel_weights, L0_attn_qkv_weight, L0_attn_proj_weight, L0_ffn_W_qkv, L0_ffn_b_qkv, L0_ffn_W_gate, L0_ffn_b_gate, L0_ffn_A, L0_ffn_B_lora, L0_ffn_W_proj, L0_ffn_b_proj):
    import jax
    import jax.numpy as jnp

    def _L0_tok_ref(x, channel_weights):
        import jax, jax.numpy as jnp
        import numpy as np
        IMG = 224
        PATCH = 16
        EMBED = 192
        C = 12
        B = 64
        Bb, Cc, H, W = x.shape
        K = PATCH
        n = H // K
        pooled = x.reshape(Bb, Cc, n, K, n, K).sum(axis=(3, 5))
        out = jnp.einsum('bcij,ce->bije', pooled, channel_weights)
        return out.reshape(Bb, n * n, EMBED)

    def _L0_attn_ref(x, qkv_weight, proj_weight):
        import jax, jax.numpy as jnp
        import numpy as np
        B, N, C = (8, 256, 192)
        H = 12
        D = C // H
        SCALE = D ** (-0.5)
        EPS = 1e-05

        def _layer_norm(x):
            mean = x.mean(-1, keepdims=True)
            var = ((x - mean) ** 2).mean(-1, keepdims=True)
            return (x - mean) / jnp.sqrt(var + EPS)
        Bx, Nx, Cx = x.shape
        qkv = x @ qkv_weight.T
        qkv = qkv.reshape(Bx, Nx, 3, H, D).transpose(2, 0, 3, 1, 4)
        q, k, v = (qkv[0], qkv[1], qkv[2])
        q = _layer_norm(q) * SCALE
        k = _layer_norm(k)
        attn = jnp.einsum('bhnd,bhmd->bhnm', q, k)
        attn = jax.nn.softmax(attn, axis=-1)
        out = jnp.einsum('bhnm,bhmd->bhnd', attn, v)
        out = out.transpose(0, 2, 1, 3).reshape(Bx, Nx, Cx)
        return out @ proj_weight.T

    def _L0_ffn_ref(x, W_qkv, b_qkv, W_gate, b_gate, A, B_lora, W_proj, b_proj):
        import jax, jax.numpy as jnp
        import numpy as np
        B_SZ, S, D = (8, 128, 192)
        H = 12
        N_EXP = 8
        RANK = 16
        ALPHA = 32
        TOP_K = 2
        b, s, d = x.shape
        n_exp, rank = (A.shape[0], A.shape[1])
        scaling = ALPHA / rank
        head_dim = d // H
        scale = head_dim ** (-0.5)
        t = b * s
        x_flat = x.reshape(t, d)
        qkv_base = x @ W_qkv.T + b_qkv
        logits = x_flat @ W_gate.T + b_gate
        router_probs = jax.nn.softmax(logits, axis=-1)
        top_k_weights, top_k_indices = jax.lax.top_k(router_probs, TOP_K)
        a_down = jnp.einsum('td,nrd->tnr', x_flat, A)
        expert_out = jnp.einsum('tnr,nor->tno', a_down, B_lora) * scaling
        dispatch = jnp.zeros((t, n_exp), x.dtype).at[jnp.arange(t)[:, None], top_k_indices].add(top_k_weights)
        sparse_out = jnp.einsum('tno,tn->to', expert_out, dispatch)
        qkv = qkv_base + sparse_out.reshape(b, s, 3 * d)
        qkv = qkv.reshape(b, s, 3, H, head_dim).transpose(2, 0, 3, 1, 4)
        q, k, v = (qkv[0], qkv[1], qkv[2])
        attn = jax.nn.softmax(jnp.einsum('bhqd,bhkd->bhqk', q, k) * scale, axis=-1)
        out = jnp.einsum('bhqk,bhkd->bhqd', attn, v)
        out = out.transpose(0, 2, 1, 3).reshape(b, s, d)
        return out @ W_proj.T + b_proj
    h = _L0_tok_ref(x, L0_tok_channel_weights)
    h = h + _L0_attn_ref(_layernorm(h, axis=-1), L0_attn_qkv_weight, L0_attn_proj_weight)
    h = h + _L0_ffn_ref(_layernorm(h, axis=-1), L0_ffn_W_qkv, L0_ffn_b_qkv, L0_ffn_W_gate, L0_ffn_b_gate, L0_ffn_A, L0_ffn_B_lora, L0_ffn_W_proj, L0_ffn_b_proj)
    return h

_drawn_inputs = setup_inputs


def setup_inputs(seed=0):
    import zlib

    import numpy as np

    out = dict(_drawn_inputs(seed))
    spreads = {'L0_ffn_b_qkv': (0.0, 0.8), 'L0_ffn_b_gate': (0.0, 0.8), 'L0_ffn_b_proj': (0.0, 2.0)}
    factors = {'L0_attn_qkv_weight': 8.0,
     'L0_attn_proj_weight': 8.0,
     'L0_ffn_W_qkv': 8.0,
     'L0_ffn_W_gate': 8.0,
     'L0_ffn_A': 8.0,
     'L0_ffn_B_lora': 8.0,
     'L0_ffn_W_proj': 8.0}
    for name, (base, spread) in spreads.items():
        noise = np.random.default_rng([zlib.crc32(name.encode()), seed]).standard_normal(out[name].shape)
        drawn = base * np.exp(spread * noise) if base else spread * noise
        out[name] = jnp.asarray(drawn.astype(out[name].dtype))
    for name, factor in factors.items():
        out[name] = (out[name] * factor).astype(out[name].dtype)
    return out
```

```python
from contextlib import ExitStack

import concourse.bass as bass
from concourse import mybir

F32 = mybir.dt.float32
BF16 = mybir.dt.bfloat16
ALU = mybir.AluOpType
ACT = mybir.ActivationFunctionType
X = mybir.AxisListType.X

BATCH, CHAN, IMG, PATCH, EMBED = 64, 12, 224, 16, 192
GRID = IMG // PATCH
TOK = GRID * GRID
HALF = TOK // 2
HEADS, HD = 12, 16
QK = 2 * EMBED
CG = CHAN // 2
ROWS = CG * PATCH
EXPERTS, RANK = 8, 16
LORA = EXPERTS * RANK
LORA_SCALE = 32 / RANK
SCALE = HD ** -0.5
EPS = 1e-5
BANK = 512
PAIRS, QUADS = HEADS // 2, HEADS // 4
PARTS = 8
Q_PART = (0, 1, 2, 0, 1, 0)
K_PART = (0, 1, 0, 1, 0, 2)
POOL_SLOTS = ((0, 0), (12, 1), (32, 2), (64, 0), (76, 1), (96, 0))
W2_LORA, W2_V, W2_GATE = QK, QK + LORA, QK + LORA + EMBED
W2_COLS = W2_GATE + EXPERTS


class Chain:

    def __init__(self, sem, steps):
        self.sem, self.steps, self.batch, self.done = sem, steps, 0, 0

    def start(self, batch):
        self.batch, self.done = batch, 0

    def link(self, eng, instruction):
        self.done += 1
        instruction.then_inc(self.sem, 1)
        eng.wait_ge(self.sem, self.batch * self.steps + self.done)

    def end(self):
        assert self.done == self.steps, (self.done, self.steps)


def build(nc, x, cw, qkv1, proj1, qkv2, bqkv2, gate, bgate, lora_a, lora_b, proj2, bproj2, out):
    with ExitStack() as ctx:
        def sb(name, shape, dt=F32):
            return ctx.enter_context(nc.sbuf_tensor(name, shape, dt))

        def sem(name):
            return ctx.enter_context(nc.semaphore(name))

        psum = ctx.enter_context(nc.psum_tensor("psum", [128, 8 * BANK], F32))

        def bank(n, count=1):
            return psum[:, n * BANK:(n + count) * BANK]

        T0, T1, S0, A0, A1 = 0, 1, 2, 6, 7

        ident = sb("ident", [128, 128])
        ident16 = sb("ident16", [128, 128], BF16)
        pool_sel = sb("pool_sel", [ROWS, 2, 128])
        pool_one = sb("pool_one", [ROWS, 2, CHAN])
        den_sel = sb("den_sel", [128, 128])
        cw_row = sb("cw_row", [CHAN, EMBED])
        cw_mid = sb("cw_mid", [CHAN, EMBED])
        cw_mean = sb("cw_mean", [CHAN, 1])
        cw_slots = sb("cw_slots", [CHAN, 128])
        cwT_slots = sb("cwT_slots", [96, 2, 128])
        part_mask = sb("part_mask", [128, 3])
        w_rep = sb("w_rep", [128, QK + 2 * EMBED])
        w_mean = sb("w_mean", [128, 2 * HEADS])
        w_hi = sb("w_hi", [128, QK + 2 * EMBED], BF16)
        w_lo = sb("w_lo", [128, QK + 2 * EMBED], BF16)
        w_rest = sb("w_rest", [128, QK + 2 * EMBED])
        w_one = sb("w_one", [128, QK + 2 * EMBED], BF16)
        nat_qkv = sb("nat_qkv", [96, 6, EMBED])
        nat_qkv2 = sb("nat_qkv2", [96, 6, EMBED])
        nat_proj = sb("nat_proj", [96, 2, 2, EMBED])
        pad_proj = sb("pad_proj", [96, 2, 2, HEADS, 32])
        nat_a = sb("nat_a", [LORA, EMBED])
        nat_gate = sb("nat_gate", [EXPERTS, EMBED])
        nat_b = sb("nat_b", [96, 6, EXPERTS, RANK])
        qkv1T = sb("qkv1T", [96, 2, 3 * EMBED])
        w_two = sb("w_two", [128, 2, W2_COLS])
        w_lora = sb("w_lora", [LORA, 3 * EMBED])
        w_proj = [sb(f"w_proj{k}", [128, QUADS, EMBED]) for k in range(2)]
        b_proj = sb("b_proj", [HALF, EMBED])
        lower = sb("lower", [HALF, EXPERTS, EXPERTS])

        x_rows = sb("x_rows", [ROWS, 2 * TOK, PATCH])
        x_half = sb("x_half", [ROWS, 2 * TOK, PATCH // 2])
        x_quarter = sb("x_quarter", [ROWS, 2 * TOK, PATCH // 4])
        row_sums = sb("row_sums", [ROWS, 2, TOK])
        pooled_rest = sb("pooled_rest", [128, TOK])
        pooled = sb("pooled", [128, TOK], BF16)

        qk_flat = [sb(f"qk_flat{k}", [HALF, 2, 2, EMBED]) for k in range(2)]
        qk_rest = sb("qk_rest", [HALF, 2, 2, EMBED])
        split = [sb(f"split{k}", [HALF, 2, 2, HEADS, PARTS * HD], BF16) for k in range(2)]
        heads = [sb(f"heads{k}", [128, HEADS, 2, TOK], BF16) for k in range(2)]
        values = [sb(f"values{k}", [128, 2, HEADS, 32]) for k in range(2)]
        probs = sb("probs", [128, 2, 4, 2 * TOK])
        attended = [sb(f"attended{k}", [128, QUADS, TOK]) for k in range(2)]
        den_inv = sb("den_inv", [128, QUADS, TOK])
        normed = [sb(f"normed{k}", [128, QUADS, TOK]) for k in range(2)]

        hv = sb("hv", [HALF, 2, 2 * EMBED])
        qk_sq = sb("qk_sq", [HALF, 2, 2, EMBED])
        sq_sum = sb("sq_sum", [HALF, 4 * HEADS])
        bn6 = sb("bn6", [HALF, 2, 6])
        gap = sb("gap", [HALF, 3, 2])
        eps_h = sb("eps_h", [HALF, 2])
        var1 = sb("var1", [HALF, 4 * HEADS + 2])
        ln1 = sb("ln1", [HALF, 4 * HEADS + 2])
        rs1 = sb("rs1", [HALF, 4 * HEADS + 2])
        nt1 = sb("nt1", [HALF, 4 * HEADS + 2])
        h2 = sb("h2", [HALF, 2, EMBED])
        bn6b = sb("bn6b", [HALF, 2, 6])
        gap2 = sb("gap2", [HALF, 3, 2])
        mean2 = sb("mean2", [HALF, 2])
        var2 = sb("var2", [HALF, 2])
        ln2 = sb("ln2", [HALF, 2])
        rs2 = sb("rs2", [HALF, 2])
        nt2 = sb("nt2", [HALF, 2])
        x2 = sb("x2", [HALF, 2, EMBED])

        x2T = sb("x2T", [128, 2, TOK])
        residual = sb("residual", [HALF, 2, EMBED])
        logits = sb("logits", [HALF, 2, EXPERTS])
        lmax = sb("lmax", [HALF, 2])
        shifted = sb("shifted", [HALF, 2, EXPERTS])
        gexp = sb("gexp", [HALF, 2, EXPERTS])
        gsum = sb("gsum", [HALF, 2])
        ginv = sb("ginv", [HALF, 2])
        beats = sb("beats", [HALF, 2, EXPERTS, EXPERTS])
        ties = sb("ties", [HALF, 2, EXPERTS, EXPERTS])
        rank = sb("rank", [HALF, 2, EXPERTS])
        dispatch = sb("dispatch", [HALF, 2, EXPERTS])
        down = sb("down", [HALF, 2, LORA])
        downT = sb("downT", [LORA, TOK])
        smax = sb("smax", [HALF, HEADS, 2])
        smax_rest = sb("smax_rest", [HALF, 2, HEADS])
        max_parts = sb("max_parts", [HALF, 2, HEADS, 32], BF16)
        result = sb("result", [HALF, 2, EMBED])

        nat_loaded = [sem(f"nat_loaded{n}") for n in range(9)]
        ident_ready = sem("ident_ready")
        masks_ready = sem("masks_ready")
        setup_pool = sem("setup_pool")
        setup_vec = sem("setup_vec")
        setup_turned = sem("setup_turned")
        setup_copied = sem("setup_copied")
        padded = sem("padded")
        cw_centred = sem("cw_centred")
        rep_done = sem("rep_done")
        w_one_ready = sem("w_one_ready")
        zeroed = sem("zeroed")

        x_loaded = sem("x_loaded")
        x_halved = sem("x_halved")
        x_quartered = sem("x_quartered")
        rows_summed = sem("rows_summed")
        pooled_raw = sem("pooled_raw")
        pooled_split = sem("pooled_split")
        first_proj = sem("first_proj")
        first_copied = sem("first_copied")
        squared = sem("squared")
        var1_ready = sem("var1_ready")
        ln1_ready = sem("ln1_ready")
        rs1_guess = sem("rs1_guess")
        rs1_ready = sem("rs1_ready")
        values1_ready = sem("values1_ready")
        split_ready = [sem(f"split_ready{k}") for k in range(2)]
        turned = [sem(f"turned{k}") for k in range(2)]
        heads_act = [sem(f"heads_act{k}") for k in range(2)]
        heads_vec = [sem(f"heads_vec{k}") for k in range(2)]
        scored = [sem(f"scored{k}") for k in range(2)]
        exped = [sem(f"exped{k}") for k in range(2)]
        gathered = [sem(f"gathered{k}") for k in range(2)]
        attended_ready = [sem(f"attended_ready{k}") for k in range(2)]
        dens_spread = [sem(f"dens_spread{k}") for k in range(2)]
        normed_ready = [sem(f"normed_ready{k}") for k in range(2)]
        projected = [sem(f"projected{k}") for k in range(2)]
        h2_ready = sem("h2_ready")
        var2_ready = sem("var2_ready")
        ln2_ready = sem("ln2_ready")
        rs2_guess = sem("rs2_guess")
        x2_ready = sem("x2_ready")
        residual_ready = sem("residual_ready")
        x2_turned = sem("x2_turned")
        x2T_ready = sem("x2T_ready")
        second_proj = sem("second_proj")
        shifted_ready = sem("shifted_ready")
        gexp_ready = sem("gexp_ready")
        down_ready = sem("down_ready")
        down_turned = sem("down_turned")
        downT_ready = sem("downT_ready")
        second_done = sem("second_done")
        second_copied = sem("second_copied")
        max_scored = sem("max_scored")
        max_taken = sem("max_taken")
        max_parts_ready = sem("max_parts_ready")
        max_turned = sem("max_turned")
        max_placed = sem("max_placed")
        result_ready = sem("result_ready")
        stored = sem("stored")
        one_steps = Chain(sem("one_steps"), 20)
        two_steps = Chain(sem("two_steps"), 17)
        pool_steps = Chain(sem("pool_steps"), 3)

        x_dram = x.rearrange("b c (i k) w -> b c k i w", k=PATCH)
        out_dram = out.rearrange("b (s p) e -> b p s e", s=2)

        block = ctx.enter_context(nc.Block())

        def iterations(eng, emit):
            emit(0, one=True, two=False, pool=True)
            emit(1, one=True, two=True, pool=True)
            with eng.Fori(2, BATCH - 1) as i:
                emit(i, one=True, two=True, pool=True)
            emit(BATCH - 1, one=True, two=True, pool=False)
            emit(BATCH, one=False, two=True, pool=False)

        @block.sync
        def _(sp):
            def load_x(b):
                for c in range(CHAN):
                    dst = x_rows[(c % CG) * PATCH:(c % CG + 1) * PATCH, (c // CG) * TOK:(c // CG + 1) * TOK, :]
                    sp.dma_start(dst.rearrange("p (i j) w -> p i (j w)", i=GRID),
                                 x_dram[b, c]).then_inc(x_loaded, 16)

            load_x(0)
            sp.dma_start(cw_row[:], cw).then_inc(nat_loaded[0], 16)
            sp.dma_start(nat_qkv[:], qkv1.rearrange("(t p) c -> p t c", p=96)).then_inc(nat_loaded[1], 16)
            for k, w in enumerate((proj1, proj2)):
                sp.dma_start(nat_proj[:, k], w.rearrange("(t p) c -> p t c", p=96)).then_inc(nat_loaded[2 + k], 16)
            sp.dma_start(nat_qkv2[:], qkv2.rearrange("(t p) c -> p t c", p=96)).then_inc(nat_loaded[4], 16)
            sp.dma_start(nat_a[:], lora_a.rearrange("n r c -> (n r) c")).then_inc(nat_loaded[5], 16)
            sp.dma_start(nat_gate[:], gate).then_inc(nat_loaded[6], 16)
            for t in range(6):
                sp.dma_start(nat_b[:, t], lora_b[:, 96 * t:96 * t + 96, :].rearrange("n p r -> p n r")
                             ).then_inc(nat_loaded[7], 16)
            sp.wait_ge(zeroed, 1)
            sp.dma_start(w_two[96:97, 1, 0:QK], bqkv2[0:QK].unsqueeze(0)).then_inc(nat_loaded[8], 16)
            sp.dma_start(w_two[96:97, 1, W2_V:W2_V + EMBED], bqkv2[QK:3 * EMBED].unsqueeze(0)).then_inc(nat_loaded[8], 16)
            sp.dma_start(w_two[96:97, 1, W2_GATE:W2_COLS], bgate.unsqueeze(0)).then_inc(nat_loaded[8], 16)
            sp.dma_start(b_proj[:], bproj2.unsqueeze(0).to_broadcast([HALF, EMBED])).then_inc(nat_loaded[8], 16)

            def emit(i, one, two, pool):
                if pool:
                    sp.wait_ge(x_halved, i + 1)
                    load_x(i + 1)
                if two:
                    sp.wait_ge(result_ready, i)
                    sp.dma_start(out_dram[i - 1], result[:]).then_inc(stored, 16)

            iterations(sp, emit)
            sp.wait_ge(stored, 16 * BATCH)

        @block.gpsimd
        def _(gp):
            nc.gpsimd.memset(ident[:], 0.0).then_inc(setup_pool, 1)
            nc.gpsimd.memset(pool_one[:], 1.0).then_inc(setup_pool, 1)
            nc.gpsimd.memset(lower[:], 1.0).then_inc(setup_pool, 1)
            nc.gpsimd.memset(den_sel[:], 1.0).then_inc(setup_pool, 1)
            gp.wait_ge(setup_pool, 4)
            nc.gpsimd.affine_select(out=ident[:], in_=ident[:], compare_op=ALU.not_equal, fill=1.0, base=0,
                                    pattern=[[-1, 128]], channel_multiplier=1).then_inc(ident_ready, 1)
            nc.gpsimd.affine_select(out=pool_one[:], in_=pool_one[:], compare_op=ALU.is_ge, fill=0.0, base=0,
                                    pattern=[[PATCH * CG, 2], [-PATCH, CHAN]], channel_multiplier=1
                                    ).then_inc(setup_pool, 1)
            nc.gpsimd.affine_select(out=lower[:], in_=lower[:], compare_op=ALU.is_gt, fill=0.0, base=0,
                                    pattern=[[1, EXPERTS], [-1, EXPERTS]], channel_multiplier=0
                                    ).then_inc(masks_ready, 1)
            nc.gpsimd.affine_select(out=den_sel[:].rearrange("p (j r) -> p j r", r=32),
                                    in_=den_sel[:].rearrange("p (j r) -> p j r", r=32),
                                    compare_op=ALU.is_equal, fill=0.0, base=-HD,
                                    pattern=[[-32, 4], [0, 32]], channel_multiplier=1
                                    ).then_inc(masks_ready, 1)
            gp.wait_ge(setup_pool, 5)
            nc.gpsimd.affine_select(out=pool_one[:], in_=pool_one[:], compare_op=ALU.is_ge, fill=0.0, base=PATCH - 1,
                                    pattern=[[-PATCH * CG, 2], [PATCH, CHAN]], channel_multiplier=-1
                                    ).then_inc(masks_ready, 1)

            def pair_sums(b):
                gp.wait_ge(x_loaded, 16 * CHAN * (b + 1))
                h = PATCH // 2
                nc.gpsimd.tensor_tensor(x_half[:], x_rows[:, :, 0:h], x_rows[:, :, h:PATCH], ALU.add
                                        ).then_inc(x_halved, 1)
                gp.wait_ge(x_halved, b + 1)
                gp.wait_ge(rows_summed, b)
                nc.gpsimd.tensor_tensor(x_quarter[:], x_half[:, :, 0:h // 2], x_half[:, :, h // 2:h], ALU.add
                                        ).then_inc(x_quartered, 1)

            pair_sums(0)

            def emit(i, one, two, pool):
                if two:
                    gp.wait_ge(h2_ready, i)
                    gp.wait_ge(result_ready, i - 1)
                    nc.gpsimd.tensor_tensor(residual[:], h2[:], b_proj[:].unsqueeze(1).to_broadcast([HALF, 2, EMBED]),
                                            ALU.add).then_inc(residual_ready, 1)
                if one:
                    gp.wait_ge(first_copied, 2 * i + 2)
                    nc.gpsimd.tensor_tensor(qk_sq[:], qk_flat[0][:], qk_flat[0][:], ALU.mult).then_inc(squared, 1)
                    gp.wait_ge(rs1_ready, i + 1)
                    nc.gpsimd.tensor_tensor(
                        values[0][0:HALF, :, :, 0:HD],
                        hv[:, :, EMBED:2 * EMBED].rearrange("p s (h d) -> p s h d", d=HD),
                        rs1[:, 4 * HEADS:].unsqueeze(2).unsqueeze(3).to_broadcast([HALF, 2, HEADS, HD]),
                        ALU.mult).then_inc(values1_ready, 1)
                if pool:
                    pair_sums(i + 1)

            gp.wait_ge(zeroed, 1)
            gp.wait_ge(nat_loaded[8], 64)
            iterations(gp, emit)

        @block.scalar
        def _(act):
            def exps(k, b):
                for p in range(PAIRS):
                    act.wait_ge(scored[k], PAIRS * b + p + 1)
                    g = p // 2
                    if g >= 2:
                        act.wait_ge(gathered[k], QUADS * b + g - 1)
                    src = bank(S0 + 2 * (p % 2), 2)[0:HALF].rearrange("p (n c) -> p n c", n=2)[:, :, 0:2 * TOK]
                    nc.scalar.activation(probs[0:HALF, (3 * k + g) % 2, 2 * (p % 2):2 * (p % 2) + 2, :], src,
                                         ACT.Exp, scale=SCALE).then_inc(exped[k], 1)

            def copy_attended(k, b):
                act.wait_ge(gathered[k], QUADS * b + QUADS)
                nc.scalar.copy(attended[k][:, 0:2, :], bank(A0)[:, 0:2 * TOK].rearrange("p (g t) -> p g t", g=2)
                               ).then_inc(attended_ready[k], 1)
                nc.scalar.copy(attended[k][:, 2, :], bank(A1)[:, 0:TOK]).then_inc(attended_ready[k], 1)

            def copy_heads(k, b):
                for u in range(0, PAIRS, 2):
                    act.wait_ge(turned[k], PAIRS * b + u + 1)
                    nc.scalar.copy(heads[k][:, 2 * u:2 * u + 2], bank(T0).bitcast(BF16)[:, 0:4 * TOK].rearrange(
                        "p (h a t) -> p h a t", h=2, a=2)).then_inc(heads_act[k], 1)

            def emit(i, one, two, pool):
                j = i - 1
                if one:
                    act.wait_ge(first_proj, i + 1)
                    act.wait_ge(values1_ready, i)
                    both = bank(S0, 4)[0:HALF].rearrange("p (s n c) -> p s n c", s=2, n=2)
                    nc.scalar.copy(hv[:], both[:, :, 1, 0:2 * EMBED]).then_inc(first_copied, 1)
                    nc.scalar.copy(qk_flat[0][:].rearrange("p a s e -> p s a e"),
                                   both[:, :, 0, 0:QK].rearrange("p s (a e) -> p s a e", a=2)
                                   ).then_inc(first_copied, 1)
                if two:
                    act.wait_ge(x2_turned, j + 1)
                    nc.scalar.copy(x2T[0:96], bank(T0)[0:96, 0:2 * TOK].rearrange("p (c t) -> p c t", c=2)
                                   ).then_inc(x2T_ready, 1)
                if one:
                    act.wait_ge(var1_ready, i + 1)
                    nc.scalar.activation(ln1[:], var1[:], ACT.Ln).then_inc(ln1_ready, 1)
                    act.wait_ge(ln1_ready, i + 1)
                    nc.scalar.activation(rs1[:], ln1[:], ACT.Exp, scale=-0.5).then_inc(rs1_guess, 1)
                if two:
                    act.wait_ge(shifted_ready, j + 1)
                    nc.scalar.activation(gexp[:], shifted[:], ACT.Exp).then_inc(gexp_ready, 1)
                if one:
                    copy_heads(0, i)
                if two:
                    act.wait_ge(down_turned, j + 1)
                    nc.scalar.copy(downT[:], bank(A1)[:, 0:TOK]).then_inc(downT_ready, 1)
                    act.wait_ge(second_done, j + 1)
                    both = bank(S0, 4)[0:HALF].rearrange("p (s n c) -> p s n c", s=2, n=2)
                    nc.scalar.copy(qk_flat[1][:].rearrange("p a s e -> p s a e"),
                                   both[:, :, 0, 0:QK].rearrange("p s (a e) -> p s a e", a=2)
                                   ).then_inc(second_copied, 1)
                    nc.scalar.copy(values[1][0:HALF, :, :, 0:HD],
                                   both[:, :, 1, 0:EMBED].rearrange("p s (h d) -> p s h d", d=HD)
                                   ).then_inc(second_copied, 1)
                if one:
                    exps(0, i)
                    copy_attended(0, i)
                if two:
                    copy_heads(1, j)
                if one:
                    act.wait_ge(var2_ready, i + 1)
                    nc.scalar.activation(ln2[:], var2[:], ACT.Ln).then_inc(ln2_ready, 1)
                    act.wait_ge(ln2_ready, i + 1)
                    nc.scalar.activation(rs2[:], ln2[:], ACT.Exp, scale=-0.5).then_inc(rs2_guess, 1)
                if two:
                    exps(1, j)
                    copy_attended(1, j)

            act.wait_ge(zeroed, 1)
            iterations(act, emit)

        turns = []
        for t in range(6):
            for c in range(2):
                turns.append((nat_loaded[1], 16, nat_qkv[:, t, 96 * c:96 * c + 96],
                              [qkv1T[:, c, 96 * t:96 * t + 96]]))
        for k in range(2):
            for t in range(2):
                for g in range(QUADS):
                    turns.append((padded, 1, pad_proj[:, k, t, 4 * g:4 * g + 4, :].rearrange("p h r -> p (h r)"),
                                  [w_proj[k][:, g, 96 * t:96 * t + 96]]))
        for t in range(6):
            for c in range(2):
                col = 96 * t if t < 4 else W2_V + 96 * (t - 4)
                turns.append((nat_loaded[4], 16, nat_qkv2[:, t, 96 * c:96 * c + 96],
                              [w_two[0:96, c, col:col + 96]]))
        for c in range(2):
            turns.append((nat_loaded[5], 16, nat_a[:, 96 * c:96 * c + 96], [w_two[0:96, c, W2_LORA:W2_V]]))
            turns.append((nat_loaded[6], 16, nat_gate[:, 96 * c:96 * c + 96], [w_two[0:96, c, W2_GATE:W2_COLS]]))
        for t in range(6):
            turns.append((nat_loaded[7], 96, nat_b[:, t].rearrange("p n r -> p (n r)"),
                          [w_lora[:, 96 * t:96 * t + 96]]))
        for c in range(2):
            turns.append((cw_centred, 1, cw_mid[:, 96 * c:96 * c + 96],
                          [cwT_slots[:, c, r:r + CHAN] for r, _ in POOL_SLOTS]))

        @block.tensor
        def _(pe):
            pe.wait_ge(ident_ready, 1)
            for n, (loaded, value, src, dsts) in enumerate(turns):
                pe.wait_ge(loaded, value)
                if n >= 2:
                    pe.wait_ge(setup_copied, n - 1)
                rows, cols = src.shape[0], src.shape[1]
                nc.tensor.transpose(bank(n % 2)[0:cols, 0:rows], src, ident[0:rows, 0:rows]).then_inc(setup_turned, 1)
            pe.wait_ge(setup_copied, len(turns))
            for c in range(2):
                nc.tensor.matmul(bank(S0)[:, 0:QK], cwT_slots[:, c], qkv1T[:, c, 0:QK], start=c == 0, stop=c == 1)
            for c in range(2):
                nc.tensor.matmul(bank(S0 + 1)[:, 0:EMBED], cwT_slots[:, c], qkv1T[:, c, QK:], start=c == 0, stop=c == 1)
            nc.tensor.matmul(bank(S0 + 2)[:, 0:EMBED], cw_slots[:], cw_row[:], start=True, stop=True
                             ).then_inc(rep_done, 1)
            pe.wait_ge(w_one_ready, 1)
            pe.wait_ge(zeroed, 1)
            pe.wait_ge(masks_ready, 3)
            pe.wait_ge(nat_loaded[8], 64)

            def pool_product(b):
                pe.wait_ge(rows_summed, b + 1)
                for c in range(2):
                    mm = nc.tensor.matmul(bank(A1)[:, 0:TOK], pool_sel[:, c], row_sums[:, c], start=c == 0, stop=c == 1)
                mm.then_inc(pooled_raw, 1)

            def first_product(b):
                pe.wait_ge(pooled_split, b + 1)
                for s in range(2):
                    lhs = pooled[:, HALF * s:HALF * s + HALF]
                    nc.tensor.matmul(bank(S0 + 2 * s)[0:HALF, 0:QK], lhs, w_one[:, 0:QK], start=True, stop=True)
                    mm = nc.tensor.matmul(bank(S0 + 2 * s + 1)[0:HALF, 0:QK], lhs, w_one[:, QK:], start=True, stop=True)
                mm.then_inc(first_proj, 1)

            def turn_heads(k, b):
                pe.wait_ge(split_ready[k], b + 1)
                for u in range(PAIRS):
                    if u >= 2:
                        if u % 2 == 0:
                            pe.wait_ge(heads_act[k], 3 * b + u // 2)
                        else:
                            pe.wait_ge(heads_vec[k], 3 * b + u // 2)
                    to = bank(T0 + u % 2).bitcast(BF16)
                    for h in range(2):
                        for a in range(2):
                            for s in range(2):
                                at = (2 * h + a) * TOK + s * HALF
                                mm = nc.tensor.transpose(to[:, at:at + HALF], split[k][:, 1 - a, s, 2 * u + h, :],
                                                         ident16[0:HALF, 0:HALF])
                    mm.then_inc(turned[k], 1)

            def gather(k, b, g):
                to = bank(A0)[:, g * TOK:g * TOK + TOK] if g < 2 else bank(A1)[:, 0:TOK]
                for s in range(2):
                    for h in range(4):
                        mm = nc.tensor.matmul(to[32 * h:32 * h + 32], values[k][:, s, 4 * g + h, :],
                                              probs[:, (3 * k + g) % 2, h, s * TOK:s * TOK + TOK],
                                              start=s == 0, stop=s == 1, skip_group_check=True)
                mm.then_inc(gathered[k], 1)

            def attend(k, b):
                for p in range(PAIRS):
                    if p >= 2:
                        pe.wait_ge(exped[k], PAIRS * b + p - 1)
                    for h in range(2):
                        for s in range(2):
                            hd = heads[k][:, 2 * p + h]
                            mm = nc.tensor.matmul(bank(S0 + 2 * (p % 2) + h)[0:HALF, s * TOK:s * TOK + TOK],
                                                  hd[:, 0, s * HALF:s * HALF + HALF], hd[:, 1, :], start=True, stop=True)
                    mm.then_inc(scored[k], 1)
                    if p >= 3 and p % 2 == 1:
                        pe.wait_ge(exped[k], PAIRS * b + p - 1)
                        gather(k, b, p // 2 - 1)
                pe.wait_ge(exped[k], PAIRS * b + PAIRS)
                gather(k, b, QUADS - 1)

            def spread(k, b):
                pe.wait_ge(attended_ready[k], 2 * b + 2)
                for g in range(QUADS):
                    to = bank(T0)[:, g * TOK:g * TOK + TOK] if g < 2 else bank(T1)[:, 0:TOK]
                    mm = nc.tensor.matmul(to, den_sel[:], attended[k][:, g], start=True, stop=True)
                mm.then_inc(dens_spread[k], 1)

            def project(k, b):
                pe.wait_ge(normed_ready[k], b + 1)
                for s in range(2):
                    for g in range(QUADS):
                        mm = nc.tensor.matmul(bank(A0)[0:HALF, s * EMBED:s * EMBED + EMBED],
                                              normed[k][:, g, s * HALF:s * HALF + HALF], w_proj[k][:, g],
                                              start=g == 0, stop=g == QUADS - 1)
                mm.then_inc(projected[k], 1)

            pool_product(0)

            def emit(i, one, two, pool):
                j = i - 1
                if one:
                    first_product(i)
                if two:
                    pe.wait_ge(x2_ready, 2 * j + 2)
                    for c in range(2):
                        for s in range(2):
                            mm = nc.tensor.transpose(bank(T0)[0:96, c * TOK + s * HALF:c * TOK + s * HALF + HALF],
                                                     x2[:, s, 96 * c:96 * c + 96], ident[0:HALF, 0:HALF])
                    mm.then_inc(x2_turned, 1)
                    pe.wait_ge(x2T_ready, j + 1)
                    if one:
                        pe.wait_ge(first_copied, 2 * i + 2)
                    for s in range(2):
                        for n, (lo, hi) in enumerate(((0, W2_V), (W2_V, W2_COLS))):
                            for c in range(2):
                                rows = 96 + c
                                mm = nc.tensor.matmul(bank(S0 + 2 * s + n)[0:HALF, 0:hi - lo],
                                                      x2T[0:rows, c, s * HALF:s * HALF + HALF],
                                                      w_two[0:rows, c, lo:hi], start=c == 0, stop=c == 1)
                    mm.then_inc(second_proj, 1)
                if one:
                    turn_heads(0, i)
                if two:
                    pe.wait_ge(down_ready, j + 1)
                    for s in range(2):
                        mm = nc.tensor.transpose(bank(A1)[:, s * HALF:s * HALF + HALF], down[:, s], ident[0:HALF, 0:HALF])
                    mm.then_inc(down_turned, 1)
                    pe.wait_ge(downT_ready, j + 1)
                    for s in range(2):
                        lhs = downT[:, s * HALF:s * HALF + HALF]
                        nc.tensor.matmul(bank(S0 + 2 * s)[0:HALF, 0:QK], lhs, w_lora[:, 0:QK], start=False, stop=True,
                                         skip_group_check=True)
                        mm = nc.tensor.matmul(bank(S0 + 2 * s + 1)[0:HALF, 0:EMBED], lhs, w_lora[:, QK:], start=False,
                                              stop=True, skip_group_check=True)
                    mm.then_inc(second_done, 1)
                if one:
                    if two:
                        pe.wait_ge(second_copied, 2 * j + 2)
                        pe.wait_ge(result_ready, j)
                    else:
                        pe.wait_ge(first_copied, 2 * i + 2)
                    pe.wait_ge(heads_act[0], 3 * i + 3)
                    pe.wait_ge(heads_vec[0], 3 * i + 3)
                    pe.wait_ge(values1_ready, i + 1)
                    attend(0, i)
                if two:
                    turn_heads(1, j)
                    pe.wait_ge(heads_act[1], 3 * j + 3)
                    pe.wait_ge(heads_vec[1], 3 * j + 3)
                    for p in range(PAIRS):
                        if p >= 2:
                            pe.wait_ge(max_taken, PAIRS * j + p - 1)
                        for h in range(2):
                            for s in range(2):
                                hd = heads[1][:, 2 * p + h]
                                mm = nc.tensor.matmul(bank(S0 + 2 * (p % 2) + h)[0:HALF, s * TOK:s * TOK + TOK],
                                                      hd[:, 1, s * HALF:s * HALF + HALF], hd[:, 0, :],
                                                      start=True, stop=True)
                        mm.then_inc(max_scored, 1)
                if one:
                    spread(0, i)
                    project(0, i)
                if pool:
                    pool_product(i + 1)
                if two:
                    pe.wait_ge(max_parts_ready, j + 1)
                    for m in range(QUADS):
                        if m >= 2:
                            pe.wait_ge(max_placed, QUADS * j + m - 1)
                        to = bank(T0 + m % 2).bitcast(BF16)
                        for h in range(4):
                            for s in range(2):
                                at = h * TOK + s * HALF
                                mm = nc.tensor.transpose(to[96:128, at:at + HALF], max_parts[:, s, 4 * m + h, :],
                                                         ident16[0:HALF, 0:HALF])
                        mm.then_inc(max_turned, 1)
                    pe.wait_ge(max_placed, QUADS * j + QUADS)
                    if one:
                        pe.wait_ge(h2_ready, i + 1)
                    if pool:
                        pe.wait_ge(pooled_split, i + 2)
                    attend(1, j)
                    spread(1, j)
                    project(1, j)

            iterations(pe, emit)

        @block.vector
        def _(dve):
            def fill(ap, value):
                nc.vector.memset(ap, value).then_inc(setup_vec, 1)
                fills[0] += 1

            fills = [0]
            for ap in (cw_slots[:], cwT_slots[:], pool_sel[:], w_two[:], split[0][:], split[1][:], values[0][:],
                       values[1][:], probs[:], max_parts[:], pad_proj[:], x2T[:]):
                fill(ap, 0.0)
            dve.wait_ge(setup_vec, fills[0])
            for k in range(2):
                fill(values[k][0:HALF, :, :, HD:HD + 1], 1.0)
            fill(split[1][:, 1, :, :, 6 * HD:6 * HD + 3], 1.0)
            fill(x2T[96:97, 1, :], 1.0)
            dve.wait_ge(setup_vec, fills[0])
            dve.wait_ge(ident_ready, 1)
            nc.vector.tensor_copy(ident16[:], ident[:]).then_inc(zeroed, 1)
            dve.wait_ge(masks_ready, 3)
            n = fills[0]
            for r, _ in POOL_SLOTS:
                nc.vector.tensor_copy(pool_sel[:, :, r:r + CHAN], pool_one[:])
                nc.vector.tensor_copy(cw_slots[:, r:r + CHAN], ident[0:CHAN, 0:CHAN])
            for part in range(3):
                spans = [ident[:, r:r + CHAN] for r, p in POOL_SLOTS if p == part]
                for m, span in enumerate(spans):
                    nc.vector.tensor_reduce(w_mean[:, 3 * part + m:3 * part + m + 1], span, X, ALU.add).then_inc(setup_vec, 1)
                    n += 1
            dve.wait_ge(setup_vec, n)
            for part in range(3):
                count = sum(p == part for _, p in POOL_SLOTS)
                nc.vector.tensor_reduce(part_mask[:, part:part + 1], w_mean[:, 3 * part:3 * part + count], X, ALU.add
                                        ).then_inc(setup_vec, 1)
                n += 1
            for k in range(2):
                dve.wait_ge(nat_loaded[2 + k], 16)
                for t in range(2):
                    ins = nc.vector.tensor_copy(pad_proj[:, k, t, :, 0:HD],
                                                nat_proj[:, k, t].rearrange("p (h d) -> p h d", d=HD))
            ins.then_inc(padded, 1)
            dve.wait_ge(nat_loaded[0], 16)
            nc.vector.tensor_reduce(cw_mean[:], cw_row[:], X, ALU.add).then_inc(setup_vec, 1)
            n += 1
            dve.wait_ge(setup_vec, n)
            nc.vector.tensor_scalar(cw_mean[:], cw_mean[:], 1.0 / EMBED, None, ALU.mult).then_inc(setup_vec, 1)
            n += 1
            dve.wait_ge(setup_vec, n)
            nc.vector.tensor_scalar(cw_mid[:], cw_row[:], cw_mean[:, 0:1], None, ALU.subtract).then_inc(cw_centred, 1)
            for m, (_, _, src, dsts) in enumerate(turns):
                dve.wait_ge(setup_turned, m + 1)
                rows, cols = src.shape[0], src.shape[1]
                for dst in dsts:
                    ins = nc.vector.tensor_copy(dst, bank(m % 2)[0:cols, 0:rows])
                ins.then_inc(setup_copied, 1)
            dve.wait_ge(rep_done, 1)
            for lo, b in ((0, S0), (QK, S0 + 2), (QK + EMBED, S0 + 1)):
                width = QK if lo == 0 else EMBED
                nc.vector.tensor_copy(w_rep[:, lo:lo + width], bank(b)[:, 0:width]).then_inc(setup_vec, 1)
                n += 1
            dve.wait_ge(setup_vec, n)
            qk_heads = w_rep[:, 0:QK].rearrange("p (h d) -> p h d", d=HD)
            nc.vector.tensor_reduce(w_mean[:], qk_heads, X, ALU.add).then_inc(setup_vec, 1)
            n += 1
            dve.wait_ge(setup_vec, n)
            nc.vector.tensor_scalar(w_mean[:], w_mean[:], 1.0 / HD, None, ALU.mult).then_inc(setup_vec, 1)
            n += 1
            dve.wait_ge(setup_vec, n)
            for step in (
                lambda: nc.vector.tensor_tensor(qk_heads, qk_heads,
                                                w_mean[:].unsqueeze(2).to_broadcast([128, 2 * HEADS, HD]), ALU.subtract),
                lambda: nc.vector.tensor_copy(w_hi[:], w_rep[:]),
                lambda: nc.vector.tensor_tensor(w_rest[:], w_rep[:], w_hi[:], ALU.subtract),
                lambda: nc.vector.tensor_scalar(w_one[:], w_hi[:], part_mask[:, 0:1], None, ALU.mult),
                lambda: nc.vector.tensor_copy(w_hi[:], w_rest[:]),
                lambda: nc.vector.tensor_tensor(w_lo[:], w_rest[:], w_hi[:], ALU.subtract),
                lambda: nc.vector.scalar_tensor_tensor(out=w_one[:], in0=w_hi[:], scalar=part_mask[:, 1:2],
                                                       in1=w_one[:], op0=ALU.mult, op1=ALU.add),
            ):
                step().then_inc(setup_vec, 1)
                n += 1
                dve.wait_ge(setup_vec, n)
            nc.vector.scalar_tensor_tensor(out=w_one[:], in0=w_lo[:], scalar=part_mask[:, 2:3], in1=w_one[:],
                                           op0=ALU.mult, op1=ALU.add).then_inc(w_one_ready, 1)

            def sum_rows(b):
                dve.wait_ge(x_quartered, b + 1)
                dve.wait_ge(pooled_raw, b)
                nc.vector.tensor_reduce(row_sums[:].rearrange("p c t -> p (c t)"), x_quarter[:], X, ALU.add
                                        ).then_inc(rows_summed, 1)

            def split_pooled(b):
                dve.wait_ge(pooled_raw, b + 1)
                pool_steps.start(b)
                raw = bank(A1)[:, 0:TOK]
                pool_steps.link(dve, nc.vector.tensor_copy(pooled[:], raw))
                pool_steps.link(dve, nc.vector.tensor_tensor(pooled_rest[:], raw, pooled[:], ALU.subtract))
                pool_steps.link(dve, nc.vector.tensor_copy(pooled[64:128], pooled_rest[64:128]))
                nc.vector.tensor_tensor(pooled[96:128], pooled_rest[96:128], pooled[96:128], ALU.subtract
                                        ).then_inc(pooled_split, 1)

            def split_qk(k, steps):
                flat = qk_flat[k][:].rearrange("p a s (h d) -> p (a s h) d", d=HD)
                rest = qk_rest[:].rearrange("p a s (h d) -> p (a s h) d", d=HD)
                slots = split[k][:].rearrange("p a s h (n d) -> p (a s h) n d", d=HD)
                n = 2 * HEADS
                q, kk = slice(0, n), slice(n, 2 * n)
                steps.link(dve, nc.vector.tensor_copy(slots[:, :, 0], flat))
                steps.link(dve, nc.vector.tensor_tensor(rest, flat, slots[:, :, 0], ALU.subtract))
                steps.link(dve, nc.vector.tensor_copy(slots[:, :, 1], rest))
                nc.vector.tensor_tensor(slots[:, q, 2], rest[:, q], slots[:, q, 1], ALU.subtract)
                nc.vector.tensor_tensor(slots[:, kk, 5], rest[:, kk], slots[:, kk, 1], ALU.subtract)
                for at, part in ((3, 0), (4, 1), (5, 0)):
                    nc.vector.tensor_copy(slots[:, q, at], slots[:, q, part])
                for at, part in ((2, 0), (3, 1), (4, 0)):
                    ins = nc.vector.tensor_copy(slots[:, kk, at], slots[:, kk, part])
                ins.then_inc(split_ready[k], 1)

            def copy_heads(k, b):
                for u in range(1, PAIRS, 2):
                    dve.wait_ge(turned[k], PAIRS * b + u + 1)
                    nc.vector.tensor_copy(heads[k][:, 2 * u:2 * u + 2].rearrange("p h a t -> p (h a t)"),
                                          bank(T1).bitcast(BF16)[:, 0:4 * TOK]).then_inc(heads_vec[k], 1)

            def normalise(k, b, steps):
                dve.wait_ge(dens_spread[k], b + 1)
                nc.vector.reciprocal(den_inv[:, 0:2], bank(T0)[:, 0:2 * TOK].rearrange("p (g t) -> p g t", g=2))
                steps.link(dve, nc.vector.reciprocal(den_inv[:, 2], bank(T1)[:, 0:TOK]))
                nc.vector.tensor_tensor(normed[k][:], attended[k][:], den_inv[:], ALU.mult
                                        ).then_inc(normed_ready[k], 1)

            def variance(steps, bn, gap, var):
                steps.link(dve, nc.vector.tensor_tensor(gap[:, 0], bn[:, :, 1], bn[:, :, 4], ALU.subtract))
                nc.vector.scalar_tensor_tensor(out=gap[:, 1], in0=gap[:, 0], scalar=0.25, in1=gap[:, 0],
                                               op0=ALU.mult, op1=ALU.mult)
                steps.link(dve, nc.vector.scalar_tensor_tensor(
                    out=gap[:, 2], in0=bn[:, :, 2], scalar=EMBED * EPS, in1=bn[:, :, 5], op0=ALU.add, op1=ALU.add))
                return nc.vector.scalar_tensor_tensor(out=var, in0=gap[:, 2], scalar=1.0 / EMBED, in1=gap[:, 1],
                                                      op0=ALU.mult, op1=ALU.add)

            def newton(steps, var, guess, tmp):
                steps.link(dve, nc.vector.tensor_tensor(tmp[:], guess[:], guess[:], ALU.mult))
                steps.link(dve, nc.vector.tensor_tensor(tmp[:], tmp[:], var[:], ALU.mult))
                steps.link(dve, nc.vector.tensor_scalar(tmp[:], tmp[:], -0.5, 1.5, ALU.mult, ALU.add))
                return nc.vector.tensor_tensor(guess[:], guess[:], tmp[:], ALU.mult)

            sum_rows(0)
            split_pooled(0)

            def emit(i, one, two, pool):
                j = i - 1
                if two:
                    two_steps.start(j)
                if one:
                    one_steps.start(i)
                    dve.wait_ge(first_copied, 2 * i + 1)
                    for s in range(2):
                        ins = nc.vector.bn_stats(bn6[:, s], hv[:, s, 0:EMBED])
                    one_steps.link(dve, ins)
                    one_steps.link(dve, variance(one_steps, bn6, gap, var1[:, 4 * HEADS:]))
                    st = var1[:, 0:4 * HEADS].rearrange("p (a s h) -> p a s h", a=2, s=2)
                    ss = sq_sum[:].rearrange("p (a s h) -> p a s h", a=2, s=2)
                    nc.vector.tensor_scalar(eps_h[:], var1[:, 4 * HEADS:], EPS, None, ALU.mult)
                    dve.wait_ge(squared, i + 1)
                    one_steps.link(dve, nc.vector.tensor_reduce(
                        sq_sum[:], qk_sq[:].rearrange("p a s (h d) -> p (a s h) d", d=HD), X, ALU.add))
                    for s in range(2):
                        ins = nc.vector.tensor_scalar(st[:, :, s], ss[:, :, s], 1.0 / HD, eps_h[:, s:s + 1],
                                                      ALU.mult, ALU.add)
                    ins.then_inc(var1_ready, 1)
                    dve.wait_ge(rs1_guess, i + 1)
                    newton(one_steps, var1, rs1, nt1).then_inc(rs1_ready, 1)
                    dve.wait_ge(rs1_ready, i + 1)
                    flat = qk_flat[0][:].rearrange("p a s (h d) -> p (a s h) d", d=HD)
                    one_steps.link(dve, nc.vector.tensor_tensor(
                        flat, flat, rs1[:, 0:4 * HEADS].unsqueeze(2).to_broadcast([HALF, 4 * HEADS, HD]), ALU.mult))
                    split_qk(0, one_steps)
                if two:
                    dve.wait_ge(second_proj, j + 1)
                    both = bank(S0, 4)[0:HALF].rearrange("p (s n c) -> p s n c", s=2, n=2)
                    two_steps.link(dve, nc.vector.tensor_copy(logits[:], both[:, :, 1, EMBED:EMBED + EXPERTS]))
                    two_steps.link(dve, nc.vector.tensor_reduce(lmax[:], logits[:], X, ALU.max))
                    nc.vector.tensor_tensor(shifted[:], logits[:], lmax[:].unsqueeze(2).to_broadcast([HALF, 2, EXPERTS]),
                                            ALU.subtract).then_inc(shifted_ready, 1)
                    full = [HALF, 2, EXPERTS, EXPERTS]
                    lj, li = logits[:].unsqueeze(2).to_broadcast(full), logits[:].unsqueeze(3).to_broadcast(full)
                    nc.vector.tensor_tensor(beats[:], lj, li, ALU.is_gt)
                    two_steps.link(dve, nc.vector.tensor_tensor(ties[:], lj, li, ALU.is_equal))
                    two_steps.link(dve, nc.vector.tensor_tensor(ties[:], ties[:], lower[:].unsqueeze(1).to_broadcast(full),
                                                                ALU.mult))
                    two_steps.link(dve, nc.vector.tensor_tensor(beats[:], beats[:], ties[:], ALU.add))
                    dve.wait_ge(gexp_ready, j + 1)
                    two_steps.link(dve, nc.vector.tensor_reduce(rank[:], beats[:], X, ALU.add))
                    two_steps.link(dve, nc.vector.tensor_reduce(gsum[:], gexp[:], X, ALU.add))
                    two_steps.link(dve, nc.vector.reciprocal(ginv[:], gsum[:]))
                    two_steps.link(dve, nc.vector.scalar_tensor_tensor(
                        out=dispatch[:], in0=rank[:], scalar=1.5, in1=gexp[:], op0=ALU.is_lt, op1=ALU.mult))
                    two_steps.link(dve, nc.vector.scalar_tensor_tensor(
                        out=dispatch[:], in0=dispatch[:], scalar=LORA_SCALE,
                        in1=ginv[:].unsqueeze(2).to_broadcast([HALF, 2, EXPERTS]), op0=ALU.mult, op1=ALU.mult))
                    nc.vector.tensor_tensor(
                        down[:].rearrange("p s (n r) -> p s n r", r=RANK),
                        both[:, :, 0, QK:QK + LORA].rearrange("p s (n r) -> p s n r", r=RANK),
                        dispatch[:].unsqueeze(3).to_broadcast([HALF, 2, EXPERTS, RANK]), ALU.mult).then_inc(down_ready, 1)
                if one:
                    copy_heads(0, i)
                if two:
                    dve.wait_ge(second_copied, 2 * j + 1)
                    split_qk(1, two_steps)
                if pool:
                    sum_rows(i + 1)
                if two:
                    copy_heads(1, j)
                    for p in range(PAIRS):
                        dve.wait_ge(max_scored, PAIRS * j + p + 1)
                        src = bank(S0 + 2 * (p % 2), 2)[0:HALF].rearrange("p (n c) -> p n c", n=2)[:, :, 0:2 * TOK]
                        nc.vector.tensor_reduce(smax[:, 2 * p:2 * p + 2], src.rearrange("p n (s t) -> p n s t", s=2),
                                                X, ALU.max).then_inc(max_taken, 1)
                    dve.wait_ge(max_taken, PAIRS * j + PAIRS)
                    mx = smax[:].rearrange("p h s -> p s h")
                    two_steps.link(dve, nc.vector.tensor_scalar(max_parts[:, :, :, 0], mx, -1.0, None, ALU.mult))
                    two_steps.link(dve, nc.vector.scalar_tensor_tensor(
                        out=smax_rest[:], in0=mx, scalar=-1.0, in1=max_parts[:, :, :, 0], op0=ALU.mult, op1=ALU.subtract))
                    two_steps.link(dve, nc.vector.tensor_copy(max_parts[:, :, :, 1], smax_rest[:]))
                    nc.vector.tensor_tensor(max_parts[:, :, :, 2], smax_rest[:], max_parts[:, :, :, 1], ALU.subtract
                                            ).then_inc(max_parts_ready, 1)
                if one:
                    normalise(0, i, one_steps)
                if two:
                    for m in range(QUADS):
                        dve.wait_ge(max_turned, QUADS * j + m + 1)
                        nc.vector.tensor_copy(heads[1][96:128, 4 * m:4 * m + 4, 1, :],
                                              bank(T0 + m % 2).bitcast(BF16)[96:128, 0:4 * TOK].rearrange(
                                                  "p (h t) -> p h t", h=4)).then_inc(max_placed, 1)
                if one:
                    dve.wait_ge(projected[0], i + 1)
                    if two:
                        dve.wait_ge(residual_ready, i)
                    nc.vector.tensor_tensor(h2[:], bank(A0)[0:HALF, 0:2 * EMBED].rearrange("p (s e) -> p s e", s=2),
                                            hv[:, :, 0:EMBED], ALU.add).then_inc(h2_ready, 1)
                    dve.wait_ge(h2_ready, i + 1)
                    for s in range(2):
                        ins = nc.vector.bn_stats(bn6b[:, s], h2[:, s])
                    one_steps.link(dve, ins)
                    variance(one_steps, bn6b, gap2, var2[:]).then_inc(var2_ready, 1)
                    nc.vector.scalar_tensor_tensor(out=mean2[:], in0=gap2[:, 0], scalar=-0.5, in1=bn6b[:, :, 1],
                                                   op0=ALU.mult, op1=ALU.add)
                    dve.wait_ge(rs2_guess, i + 1)
                    one_steps.link(dve, newton(one_steps, var2, rs2, nt2))
                    for s in range(2):
                        nc.vector.tensor_scalar(x2[:, s], h2[:, s], mean2[:, s:s + 1], rs2[:, s:s + 1],
                                                ALU.subtract, ALU.mult).then_inc(x2_ready, 1)
                    one_steps.end()
                if pool:
                    split_pooled(i + 1)
                if two:
                    normalise(1, j, two_steps)
                    two_steps.end()
                    dve.wait_ge(projected[1], j + 1)
                    dve.wait_ge(residual_ready, j + 1)
                    dve.wait_ge(stored, 16 * j)
                    nc.vector.tensor_tensor(result[:], bank(A0)[0:HALF, 0:2 * EMBED].rearrange("p (s e) -> p s e", s=2),
                                            residual[:], ALU.add).then_inc(result_ready, 1)

            iterations(dve, emit)


_INS = ["x", "L0_tok_channel_weights", "L0_attn_qkv_weight", "L0_attn_proj_weight", "L0_ffn_W_qkv", "L0_ffn_b_qkv",
        "L0_ffn_W_gate", "L0_ffn_b_gate", "L0_ffn_A", "L0_ffn_B_lora", "L0_ffn_W_proj", "L0_ffn_b_proj"]
_OUTS = [((BATCH, TOK, EMBED), "float32")]


def kernel(**inputs):
    import numpy as _np
    import concourse.bacc as _bacc
    from concourse import mybir as _mybir
    from concourse.bass_utils import run_bass_kernel_spmd as _run

    nc = _bacc.Bacc("TRN2", target_bir_lowering=False, num_devices=1)
    arrays, args = {}, []
    for name in _INS:
        a = _np.ascontiguousarray(inputs[name])
        arrays[f"in_{name}_dram"] = a
        args.append(nc.dram_tensor(f"in_{name}_dram", a.shape, _mybir.dt.from_np(a.dtype), kind="ExternalInput").ap())
    for i, (shape, dtype) in enumerate(_OUTS):
        dt = _mybir.dt.from_np(_np.dtype(dtype))
        args.append(nc.dram_tensor(f"out_{i}_dram", shape, dt, kind="ExternalOutput").ap())
    build(nc, *args)
    r = _run(nc, [arrays], core_ids=[0])
    return r.results[0]["out_0_dram"]
```

```python
from contextlib import ExitStack

import concourse.bass as bass
from concourse import mybir

F32 = mybir.dt.float32
BF16 = mybir.dt.bfloat16
I32 = mybir.dt.int32
ALU = mybir.AluOpType
ACT = mybir.ActivationFunctionType
X = mybir.AxisListType.X

BATCH, CHAN, IMG, PATCH, EMBED = 64, 12, 224, 16, 192
GRID = IMG // PATCH
TOK = GRID * GRID
HALF = TOK // 2
HEADS, HD = 12, 16
QK = 2 * EMBED
CG = CHAN // 2
ROWS = CG * PATCH
EXPERTS, RANK = 8, 16
LORA = EXPERTS * RANK
LORA_SCALE = 32 / RANK
SCALE = HD ** -0.5
EPS = 1e-5
BANK = 512
PAIRS, QUADS = HEADS // 2, HEADS // 4
PARTS = 8
POOL_SLOTS = ((0, 0), (12, 1), (32, 2), (64, 0), (76, 1), (96, 0))
W2_V, W2_LORA, W2_GATE = QK, QK + EMBED, QK + EMBED + LORA
W2_COLS = W2_GATE + EXPERTS
STAGES = 5
RSQRT_GUESS = 0x5F3759DF

ACT_COPIES = (0, 2, 4)

ORDER = {
    "pe": """
2t0 5a0 5a1 2t1 2t2 5a2 5a3 2t3 2t4 1p0 2t5 1p1 4t0 4t1 5e0 5a4 5a5 4t2 4t3 2a0 5e1 2a1 5g 2a2 4t4 4t5 2a3
2e0 2a4 5n 2a5 4b0 3x 4b1 2e1 4b2 3g 5m 2g 4b3 4b4 5o 3d 4b5 2n 3q0 3v0 4u0 4u1 3q1 2m 3v1 0p 4u2 2o
""".split(),
    "act": """
2t0 5a0 5a1 2t2 5a2 5a3 2t4 1p0 1p1 4t0 5a4 5a5 4t2 2a0 2a1 5g 2a2 4t4 2a3 2a4 2a5 3x 3g 5m 2g 3d 1c 3q0 3v0
4u0 4u1 3q1 2m 3v1 3c 4u2
""".split(),
    "vec": """
2t1 2t3 2t5 4t1 1s 4t3 1f 4t5 3l 5n 4b0 4b1 4b2 3g 4b3 4b4 4b5 5o 4k 2n 1w 0q 1z 0p 3w 2o 3z
""".split(),
    "pool": """
2r 2v 5r 5v 4r 4v 0q0 0q1 1h 0q2 1y 3x 3y
""".split(),
    "sync": """
0q 5o
""".split(),
}


class Chain:

    def __init__(self, sem, steps):
        self.sem, self.steps, self.batch, self.done = sem, steps, 0, 0

    def start(self, batch):
        self.batch, self.done = batch, 0

    def link(self, eng, instruction):
        self.done += 1
        instruction.then_inc(self.sem, 1)
        eng.wait_ge(self.sem, self.batch * self.steps + self.done)

    def end(self):
        assert self.done == self.steps, (self.done, self.steps)


class Bank:

    def __init__(self):
        self.reads, self.before = [], False

    def take(self, pe, i, reads):
        for sem, per, count, stage in self.reads:
            pe.wait_ge(sem, per * (i - stage + (0 if self.before else 1)) + count)
        self.reads, self.before = reads, False


def build(nc, x, cw, qkv1, proj1, qkv2, bqkv2, gate, bgate, lora_a, lora_b, proj2, bproj2, out):
    with ExitStack() as ctx:
        def sb(name, shape, dt=F32):
            return ctx.enter_context(nc.sbuf_tensor(name, shape, dt))

        def sem(name):
            return ctx.enter_context(nc.semaphore(name))

        psum = ctx.enter_context(nc.psum_tensor("psum", [128, 8 * BANK], F32))

        def bank(n, count=1):
            return psum[:, n * BANK:(n + count) * BANK]

        T0, T1, S0, A0, A1 = 0, 1, 2, 6, 7

        ident = sb("ident", [128, 128])
        ident16 = sb("ident16", [128, 128], BF16)
        pool_sel = sb("pool_sel", [ROWS, 2, 128])
        pool_one = sb("pool_one", [ROWS, 2, CHAN])
        cw_row = sb("cw_row", [CHAN, EMBED])
        cw_mid = sb("cw_mid", [CHAN, EMBED])
        cw_mean = sb("cw_mean", [CHAN, 1])
        cw_slots = sb("cw_slots", [CHAN, 128])
        cwT_slots = sb("cwT_slots", [96, 2, 128])
        part_mask = sb("part_mask", [128, 3])
        w_mean = sb("w_mean", [128, 2 * HEADS])
        w_hi = sb("w_hi", [128, QK + 2 * EMBED], BF16)
        w_lo = sb("w_lo", [128, QK + 2 * EMBED], BF16)
        w_one = sb("w_one", [128, QK + 2 * EMBED], BF16)
        nat_proj = sb("nat_proj", [96, 2, 2, EMBED])
        nat_a = sb("nat_a", [LORA, EMBED])
        nat_gate = sb("nat_gate", [EXPERTS, EMBED])
        nat_b = sb("nat_b", [96, 6, EXPERTS, RANK])
        qkv1T = sb("qkv1T", [96, 2, 3 * EMBED])
        w_two = sb("w_two", [128, 2, W2_COLS])
        w_lora = sb("w_lora", [LORA, 3 * EMBED])
        w_proj = [sb(f"w_proj{k}", [96, 2, EMBED]) for k in range(2)]
        b_proj = sb("b_proj", [HALF, EMBED])
        lower = sb("lower", [HALF, EXPERTS, EXPERTS])

        x_rows = sb("x_rows", [ROWS, 2 * TOK, PATCH])
        x_half = sb("x_half", [ROWS, 2 * TOK, PATCH // 2])
        x_quarter = sb("x_quarter", [ROWS, 2 * TOK, PATCH // 4])
        row_sums = sb("row_sums", [ROWS, 2, TOK])
        pooled_rest = sb("pooled_rest", [128, TOK])
        pooled = sb("pooled", [128, TOK], BF16)

        qk_flat = [sb(f"qk_flat{k}", [HALF, 2, 2, EMBED]) for k in range(2)]
        qk_rest = [sb(f"qk_rest{k}", [HALF, 2, 2, EMBED]) for k in range(2)]
        split = [sb(f"split{k}", [HALF, 2, 2, HEADS, PARTS * HD], BF16) for k in range(2)]
        heads = [sb(f"heads{k}", [128, HEADS, 2, TOK], BF16) for k in range(2)]
        raw = heads[1][:].rearrange("p h a t -> p (h a t)").bitcast(F32)
        nat_qkv, nat_qkv2 = (raw[0:96, n * 6 * EMBED:(n + 1) * 6 * EMBED].rearrange("p (t c) -> p t c", t=6)
                             for n in range(2))
        values = [sb(f"values{k}", [128, 2, HEADS, 32]) for k in range(2)]
        probs = [sb(f"probs{k}", [128, 2, 4, 2 * TOK]) for k in range(2)]
        scratch = probs[1][:].rearrange("p a b t -> p (a b t)")
        w_rep, w_rest = (scratch[:, n * (QK + 2 * EMBED):(n + 1) * (QK + 2 * EMBED)] for n in range(2))
        attended = [sb(f"attended{k}", [128, QUADS, TOK]) for k in range(2)]
        den_inv = [sb(f"den_inv{k}", [HALF, 2, HEADS]) for k in range(2)]
        normed = [sb(f"normed{k}", [HALF, 2, EMBED]) for k in range(2)]
        normedT = [sb(f"normedT{k}", [96, 2, TOK]) for k in range(2)]

        hv = sb("hv", [HALF, 2, 2 * EMBED])
        h_kept = sb("h_kept", [HALF, 2, EMBED])
        qk_sq = sb("qk_sq", [HALF, 2, 2, EMBED])
        sq_sum = sb("sq_sum", [HALF, 4 * HEADS])
        bn6 = sb("bn6", [HALF, 4, 6])
        gap = sb("gap", [HALF, 3, 4])
        var1 = sb("var1", [HALF, 4 * HEADS + 4])
        rs1 = sb("rs1", [HALF, 4 * HEADS + 4])
        nt1 = sb("nt1", [HALF, 4 * HEADS + 4])
        h2 = sb("h2", [HALF, 2, EMBED])
        mean2 = sb("mean2", [HALF, 2])
        x2 = sb("x2", [HALF, 2, EMBED])

        x2T = sb("x2T", [128, 2, TOK])
        residual2 = sb("residual2", [HALF, 2, EMBED])
        residual4 = sb("residual4", [HALF, 2, EMBED])
        residual = sb("residual", [HALF, 2, EMBED])
        nothing = sb("nothing", [HALF, HEADS])
        v_flat = sb("v_flat", [HALF, 2, EMBED])
        v_kept = sb("v_kept", [HALF, 2, EMBED])
        logits = sb("logits", [HALF, 2, EXPERTS])
        lmax = sb("lmax", [HALF, 2])
        shifted = sb("shifted", [HALF, 2, EXPERTS])
        gexp = sb("gexp", [HALF, 2, EXPERTS])
        gsum = sb("gsum", [HALF, 2])
        ginv = sb("ginv", [HALF, 2])
        beats = sb("beats", [HALF, 2, EXPERTS, 2 * EXPERTS])
        ties = sb("ties", [HALF, 2, EXPERTS, EXPERTS])
        rank = sb("rank", [HALF, 2, EXPERTS])
        dispatch = sb("dispatch", [HALF, 2, EXPERTS])
        down = sb("down", [HALF, 2, LORA])
        downT = sb("downT", [LORA, TOK])
        smax = sb("smax", [HALF, HEADS, 2])
        smax_rest = sb("smax_rest", [HALF, 2, HEADS])
        max_parts = sb("max_parts", [HALF, 2, HEADS, 32], BF16)
        result = sb("result", [HALF, 2, EMBED])

        nat_loaded = [sem(f"nat_loaded{n}") for n in range(9)]
        ident_ready = sem("ident_ready")
        masks_ready = sem("masks_ready")
        setup_pool = sem("setup_pool")
        pool_filled = sem("pool_filled")
        setup_vec = sem("setup_vec")
        setup_turned = sem("setup_turned")
        setup_copied = sem("setup_copied")
        cw_centred = sem("cw_centred")
        rep_done = sem("rep_done")
        w_one_ready = sem("w_one_ready")
        zeroed = sem("zeroed")

        x_loaded = sem("x_loaded")
        x_halved = sem("x_halved")
        x_quartered = sem("x_quartered")
        rows_summed = sem("rows_summed")
        pooled_raw = sem("pooled_raw")
        pooled_split = sem("pooled_split")
        first_proj = sem("first_proj")
        values1_ready = sem("values1_ready")
        rs1_ready = sem("rs1_ready")
        scaled = sem("scaled")
        hi_ready = [sem(f"hi_ready{k}") for k in range(2)]
        rest_ready = [sem(f"rest_ready{k}") for k in range(2)]
        mid_ready = [sem(f"mid_ready{k}") for k in range(2)]
        lo_ready = [sem(f"lo_ready{k}") for k in range(2)]
        split_ready = [sem(f"split_ready{k}") for k in range(2)]
        turned = [sem(f"turned{k}") for k in range(2)]
        scored = [sem(f"scored{k}") for k in range(2)]
        gathered = [sem(f"gathered{k}") for k in range(2)]
        attended_turned = [sem(f"attended_turned{k}") for k in range(2)]
        normed_ready = [sem(f"normed_ready{k}") for k in range(2)]
        normed_turned = [sem(f"normed_turned{k}") for k in range(2)]
        projected = [sem(f"projected{k}") for k in range(2)]
        h2_ready = sem("h2_ready")
        x2_ready = sem("x2_ready")
        x2_turned = sem("x2_turned")
        gated = sem("gated")
        shifted_ready = sem("shifted_ready")
        gexp_ready = sem("gexp_ready")
        down_ready = sem("down_ready")
        down_turned = sem("down_turned")
        second_qk_done = sem("second_qk_done")
        second_v_done = sem("second_v_done")
        residual2_ready = sem("residual2_ready")
        residual4_ready = sem("residual4_ready")
        h_kept_ready = sem("h_kept_ready")
        v_kept_ready = sem("v_kept_ready")
        residual_ready = sem("residual_ready")
        values2_ready = sem("values2_ready")
        max_scored = sem("max_scored")
        max_parts_ready = sem("max_parts_ready")
        max_turned = sem("max_turned")
        result_ready = sem("result_ready")
        stored = sem("stored")
        heads_act = [sem(f"heads_act{k}") for k in range(2)]
        heads_vec = [sem(f"heads_vec{k}") for k in range(2)]
        exped = [sem(f"exped{k}") for k in range(2)]
        attended_ready = [sem(f"attended_ready{k}") for k in range(2)]
        normedT_ready = [sem(f"normedT_ready{k}") for k in range(2)]
        x2T_ready = sem("x2T_ready")
        downT_ready = sem("downT_ready")
        max_placed = sem("max_placed")
        hv_copied = sem("hv_copied")
        qk1_copied = sem("qk1_copied")
        qk2_copied = sem("qk2_copied")
        v_copied = sem("v_copied")
        squared = sem("squared")
        max_taken = sem("max_taken")
        norm_steps = Chain(sem("norm_steps"), 14)
        last_norm_steps = Chain(sem("last_norm_steps"), 13)
        two_steps = Chain(sem("two_steps"), 1)
        three_steps = Chain(sem("three_steps"), 6)
        four_steps = Chain(sem("four_steps"), 3)
        five_steps = Chain(sem("five_steps"), 1)
        pool_steps = Chain(sem("pool_steps"), 3)

        LN1, LN2 = 4 * HEADS, 4 * HEADS + 2
        x_dram = x.rearrange("b c (i k) w -> b c k i w", k=PATCH)
        out_dram = out.rearrange("b (s p) e -> b p s e", s=2)

        block = ctx.enter_context(nc.Block())

        def slots_of(k):
            n = 2 * HEADS
            return (split[k][:].rearrange("p a s h (n d) -> p (a s h) n d", d=HD), slice(0, n), slice(n, 2 * n),
                    qk_flat[k][:].rearrange("p a s (h d) -> p (a s h) d", d=HD),
                    qk_rest[k][:].rearrange("p a s (h d) -> p (a s h) d", d=HD))

        def heads_free(eng, k, b, u):
            if not (isinstance(b, int) and b == 0):
                eng.wait_ge(scored[k], PAIRS * (b - 1) + u + 1)

        def iterations(eng, order, steps, banks=()):
            def emit(i, stages, pool):
                for bank_ in banks:
                    bank_.before = True
                for name in ORDER[order]:
                    if name[0] == "0":
                        if pool:
                            steps(name, i, i + 1)
                    elif int(name[0]) in stages:
                        steps(name, i, i - int(name[0]) + 1)

            for i in range(STAGES):
                emit(i, range(1, i + 2), True)
            with eng.Fori(STAGES, BATCH - 1) as i:
                emit(i, range(1, STAGES + 1), True)
            for i in range(BATCH - 1, BATCH + STAGES - 1):
                emit(i, range(max(1, i - BATCH + 2), STAGES + 1), False)

        @block.sync
        def _(sp):
            def load_x(b):
                for c in range(CHAN):
                    dst = x_rows[(c % CG) * PATCH:(c % CG + 1) * PATCH, (c // CG) * TOK:(c // CG + 1) * TOK, :]
                    sp.dma_start(dst.rearrange("p (i j) w -> p i (j w)", i=GRID),
                                 x_dram[b, c]).then_inc(x_loaded, 16)

            sp.dma_start(cw_row[:], cw).then_inc(nat_loaded[0], 16)
            sp.dma_start(nat_qkv, qkv1.rearrange("(t p) c -> p t c", p=96)).then_inc(nat_loaded[1], 16)
            for k, w in enumerate((proj1, proj2)):
                sp.dma_start(nat_proj[:, k], w.rearrange("(t p) c -> p t c", p=96)).then_inc(nat_loaded[2 + k], 16)
            sp.dma_start(nat_qkv2, qkv2.rearrange("(t p) c -> p t c", p=96)).then_inc(nat_loaded[4], 16)
            sp.dma_start(nat_a[:], lora_a.rearrange("n r c -> (n r) c")).then_inc(nat_loaded[5], 16)
            sp.dma_start(nat_gate[:], gate).then_inc(nat_loaded[6], 16)
            for t in range(6):
                sp.dma_start(nat_b[:, t], lora_b[:, 96 * t:96 * t + 96, :].rearrange("n p r -> p n r")
                             ).then_inc(nat_loaded[7], 16)
            load_x(0)
            sp.wait_ge(zeroed, 1)
            sp.dma_start(w_two[96:97, 1, 0:QK], bqkv2[0:QK].unsqueeze(0)).then_inc(nat_loaded[8], 16)
            sp.dma_start(w_two[96:97, 1, W2_V:W2_V + EMBED], bqkv2[QK:3 * EMBED].unsqueeze(0)).then_inc(nat_loaded[8], 16)
            sp.dma_start(w_two[96:97, 1, W2_GATE:W2_COLS], bgate.unsqueeze(0)).then_inc(nat_loaded[8], 16)
            sp.dma_start(b_proj[:], bproj2.unsqueeze(0).to_broadcast([HALF, EMBED])).then_inc(nat_loaded[8], 16)

            def steps(name, i, b):
                if name == "0q":
                    sp.wait_ge(x_halved, 2 * b)
                    load_x(b)
                if name == "5o":
                    sp.wait_ge(result_ready, b + 1)
                    sp.dma_start(out_dram[b], result[:]).then_inc(stored, 16)

            iterations(sp, "sync", steps)
            sp.wait_ge(stored, 16 * BATCH)

        @block.gpsimd
        def _(gp):
            nc.gpsimd.memset(ident[:], 0.0).then_inc(setup_pool, 1)
            nc.gpsimd.memset(pool_one[:], 1.0).then_inc(setup_pool, 1)
            nc.gpsimd.memset(lower[:], 1.0).then_inc(setup_pool, 1)
            gp.wait_ge(setup_pool, 3)
            nc.gpsimd.affine_select(out=ident[:], in_=ident[:], compare_op=ALU.not_equal, fill=1.0, base=0,
                                    pattern=[[-1, 128]], channel_multiplier=1).then_inc(ident_ready, 1)
            nc.gpsimd.affine_select(out=pool_one[:], in_=pool_one[:], compare_op=ALU.is_ge, fill=0.0, base=0,
                                    pattern=[[PATCH * CG, 2], [-PATCH, CHAN]], channel_multiplier=1
                                    ).then_inc(setup_pool, 1)
            nc.gpsimd.affine_select(out=lower[:], in_=lower[:], compare_op=ALU.is_gt, fill=0.0, base=0,
                                    pattern=[[1, EXPERTS], [-1, EXPERTS]], channel_multiplier=0
                                    ).then_inc(masks_ready, 1)
            for ap in (probs[0],):
                nc.gpsimd.memset(ap[:], 0.0).then_inc(pool_filled, 1)
            gp.wait_ge(setup_pool, 4)
            nc.gpsimd.affine_select(out=pool_one[:], in_=pool_one[:], compare_op=ALU.is_ge, fill=0.0, base=PATCH - 1,
                                    pattern=[[-PATCH * CG, 2], [PATCH, CHAN]], channel_multiplier=-1
                                    ).then_inc(masks_ready, 1)

            def pair_sums(b, part):
                h = PATCH // 2
                if part < 2:
                    if part == 0:
                        gp.wait_ge(x_loaded, 16 * CHAN * (b + 1))
                        gp.wait_ge(x_quartered, b)
                    at = slice(part * TOK, part * TOK + TOK)
                    nc.gpsimd.tensor_tensor(x_half[:, at], x_rows[:, at, 0:h], x_rows[:, at, h:PATCH], ALU.add
                                            ).then_inc(x_halved, 1)
                    return
                gp.wait_ge(x_halved, 2 * b + 2)
                gp.wait_ge(rows_summed, b)
                nc.gpsimd.tensor_tensor(x_quarter[:], x_half[:, :, 0:h // 2], x_half[:, :, h // 2:h], ALU.add
                                        ).then_inc(x_quartered, 1)

            def steps(name, i, b):
                k, part = int(name[0]) // 3, name[1]
                add, zero = nc.gpsimd.tensor_tensor, nothing[:, 0:1].unsqueeze(2).to_broadcast([HALF, 2, EMBED])
                if name == "2r":
                    gp.wait_ge(hv_copied, 2 * b + 2)
                    gp.wait_ge(h2_ready, b)
                    add(h_kept[:], hv[:, :, 0:EMBED], zero, ALU.add).then_inc(h_kept_ready, 1)
                if name == "2v":
                    gp.wait_ge(rs1_ready, b + 1)
                    gp.wait_ge(gathered[0], QUADS * b)
                    nc.gpsimd.tensor_tensor(
                        values[0][0:HALF, :, :, 0:HD],
                        hv[:, :, EMBED:2 * EMBED].rearrange("p s (h d) -> p s h d", d=HD),
                        rs1[:, LN1:LN2].unsqueeze(2).unsqueeze(3).to_broadcast([HALF, 2, HEADS, HD]),
                        ALU.mult).then_inc(values1_ready, 1)
                if name == "3x":
                    gp.wait_ge(h2_ready, b + 1)
                    gp.wait_ge(residual4_ready, b)
                    add(residual2[:], h2[:], zero, ALU.add).then_inc(residual2_ready, 1)
                if name == "4r":
                    gp.wait_ge(residual2_ready, b + 1)
                    gp.wait_ge(residual_ready, b)
                    add(residual4[:], residual2[:], b_proj[:].unsqueeze(1).to_broadcast([HALF, 2, EMBED]),
                        ALU.add).then_inc(residual4_ready, 1)
                if name == "4v":
                    gp.wait_ge(v_copied, 2 * b + 2)
                    gp.wait_ge(values2_ready, b)
                    add(v_kept[:], v_flat[:], zero, ALU.add).then_inc(v_kept_ready, 1)
                if name == "5r":
                    gp.wait_ge(residual4_ready, b + 1)
                    gp.wait_ge(result_ready, b)
                    add(residual[:], residual4[:], zero, ALU.add).then_inc(residual_ready, 1)
                if name == "5v":
                    gp.wait_ge(v_kept_ready, b + 1)
                    gp.wait_ge(gathered[1], QUADS * b)
                    add(values[1][0:HALF, :, :, 0:HD], v_kept[:].rearrange("p s (h d) -> p s h d", d=HD),
                        nothing[:].unsqueeze(1).unsqueeze(3).to_broadcast([HALF, 2, HEADS, HD]),
                        ALU.add).then_inc(values2_ready, 1)
                if name == "1h":
                    gp.wait_ge(rs1_ready, b + 1)
                    gp.wait_ge(qk1_copied, 2 * b + 2)
                    flat = slots_of(0)[3]
                    nc.gpsimd.tensor_tensor(flat, flat, rs1[:, 0:LN1].unsqueeze(2).to_broadcast([HALF, 4 * HEADS, HD]),
                                            ALU.mult).then_inc(scaled, 1)
                if part == "y":
                    slots, q, kk, _, rest = slots_of(k)
                    gp.wait_ge(mid_ready[k], b + 1)
                    for rows, at in ((q, 2), (kk, 5)):
                        nc.gpsimd.tensor_tensor(slots[:, rows, at], rest[:, rows], slots[:, rows, 1], ALU.subtract
                                                ).then_inc(lo_ready[k], 1)
                if name[:2] == "0q":
                    pair_sums(b, int(name[2]))

            for part in range(3):
                pair_sums(0, part)
            gp.wait_ge(zeroed, 1)
            gp.wait_ge(nat_loaded[8], 64)
            iterations(gp, "pool", steps)

        @block.scalar
        def _(act):
            def exps(k, b, p):
                act.wait_ge(scored[k], PAIRS * b + p + 1)
                g = p // 2
                if g >= 2:
                    act.wait_ge(gathered[k], QUADS * b + g - 1)
                src = bank(S0 + 2 * (p % 2), 2)[0:HALF].rearrange("p (n c) -> p n c", n=2)[:, :, 0:2 * TOK]
                nc.scalar.activation(probs[k][0:HALF, g % 2, 2 * (p % 2):2 * (p % 2) + 2, :], src,
                                     ACT.Exp, scale=SCALE).then_inc(exped[k], 1)

            def copy_attended(k, b):
                act.wait_ge(gathered[k], QUADS * b + QUADS)
                nc.scalar.copy(attended[k][:, 0:2, :], bank(A0)[:, 0:2 * TOK].rearrange("p (g t) -> p g t", g=2)
                               ).then_inc(attended_ready[k], 1)
                nc.scalar.copy(attended[k][:, 2, :], bank(A1)[:, 0:TOK]).then_inc(attended_ready[k], 1)

            def copy_heads(k, b, u):
                act.wait_ge(turned[k], PAIRS * b + u + 1)
                heads_free(act, k, b, u)
                nc.scalar.copy(heads[k][:, 2 * u:2 * u + 2].rearrange("p h a t -> p (h a t)"),
                               bank(T0 + u % 2).bitcast(BF16)[:, 0:4 * TOK]).then_inc(heads_act[k], 1)

            def steps(name, i, b):
                k = int(name[0]) // 3
                part = name[1]
                n = int(name[2]) if len(name) > 2 else 0
                both = bank(S0 + 2 * (n % 2), 2)[0:HALF].rearrange("p (n c) -> p n c", n=2)
                qk_bank = both[:, 0, 0:QK].rearrange("p (a e) -> p a e", a=2)
                if part == "p":
                    act.wait_ge(first_proj, 2 * b + n + 1)
                    act.wait_ge(rest_ready[0], b)
                    nc.scalar.copy(qk_flat[0][:, :, n], qk_bank).then_inc(qk1_copied, 1)
                    nc.scalar.activation(qk_sq[:, :, n], qk_bank, ACT.Square).then_inc(squared, 1)
                    act.wait_ge(values1_ready, b)
                    act.wait_ge(h_kept_ready, b)
                    nc.scalar.copy(hv[:, n], both[:, 1, 0:2 * EMBED]).then_inc(hv_copied, 1)
                if name == "3x":
                    act.wait_ge(x2_turned, b + 1)
                    nc.scalar.copy(x2T[0:96], bank(T0)[0:96, 0:2 * TOK].rearrange("p (c t) -> p c t", c=2)
                                   ).then_inc(x2T_ready, 1)
                if name == "3g":
                    act.wait_ge(shifted_ready, b + 1)
                    nc.scalar.activation(gexp[:], shifted[:], ACT.Exp).then_inc(gexp_ready, 1)
                if name == "3d":
                    act.wait_ge(down_turned, b + 1)
                    nc.scalar.copy(downT[:], bank(T0)[:, 0:TOK]).then_inc(downT_ready, 1)
                if part == "q":
                    act.wait_ge(second_qk_done, 2 * b + n + 1)
                    act.wait_ge(rest_ready[1], b)
                    nc.scalar.copy(qk_flat[1][:, :, n], qk_bank).then_inc(qk2_copied, 1)
                if part == "v":
                    act.wait_ge(second_v_done, 2 * b + n + 1)
                    act.wait_ge(v_kept_ready, b)
                    nc.scalar.copy(v_flat[:, n], both[:, 1, 0:EMBED]).then_inc(v_copied, 1)
                if part == "c":
                    act.wait_ge((scaled, qk2_copied)[k], (k + 1) * (b + 1))
                    act.wait_ge(turned[k], PAIRS * b)
                    slots, _, _, flat, _ = slots_of(k)
                    nc.scalar.copy(slots[:, :, 0], flat).then_inc(hi_ready[k], 1)
                if part == "u":
                    act.wait_ge(max_turned, QUADS * b + n + 1)
                    nc.scalar.copy(heads[1][96:128, 4 * n:4 * n + 4, 1, :],
                                   bank(T0 + n % 2).bitcast(BF16)[96:128, 0:4 * TOK].rearrange(
                                       "p (h t) -> p h t", h=4)).then_inc(max_placed, 1)
                if part == "t" and n in ACT_COPIES:
                    copy_heads(k, b, n)
                if part == "a":
                    exps(k, b, n)
                if name in ("2g", "5g"):
                    copy_attended(k, b)
                if part == "m":
                    act.wait_ge(normed_turned[k], b + 1)
                    nc.scalar.copy(normedT[k][:], bank(T0)[0:96, 0:2 * TOK].rearrange("p (c t) -> p c t", c=2)
                                   ).then_inc(normedT_ready[k], 1)

            act.wait_ge(zeroed, 1)
            iterations(act, "act", steps)

        turns = []
        for t in range(6):
            for c in range(2):
                turns.append((nat_loaded[1], 16, nat_qkv[:, t, 96 * c:96 * c + 96],
                              [qkv1T[:, c, 96 * t:96 * t + 96]]))
        for k in range(2):
            for t in range(2):
                for c in range(2):
                    turns.append((nat_loaded[2 + k], 16, nat_proj[:, k, t, 96 * c:96 * c + 96],
                                  [w_proj[k][:, c, 96 * t:96 * t + 96]]))
        for t in range(6):
            for c in range(2):
                turns.append((nat_loaded[4], 16, nat_qkv2[:, t, 96 * c:96 * c + 96],
                              [w_two[0:96, c, 96 * t:96 * t + 96]]))
        for c in range(2):
            turns.append((nat_loaded[5], 16, nat_a[:, 96 * c:96 * c + 96], [w_two[0:96, c, W2_LORA:W2_GATE]]))
            turns.append((nat_loaded[6], 16, nat_gate[:, 96 * c:96 * c + 96], [w_two[0:96, c, W2_GATE:W2_COLS]]))
        for t in range(6):
            turns.append((nat_loaded[7], 96, nat_b[:, t].rearrange("p n r -> p (n r)"),
                          [w_lora[:, 96 * t:96 * t + 96]]))
        for c in range(2):
            turns.append((cw_centred, 1, cw_mid[:, 96 * c:96 * c + 96],
                          [cwT_slots[:, c, r:r + CHAN] for r, _ in POOL_SLOTS]))

        @block.tensor
        def _(pe):
            pe.wait_ge(ident_ready, 1)
            for n, (loaded, value, src, dsts) in enumerate(turns):
                pe.wait_ge(loaded, value)
                if n >= 8:
                    pe.wait_ge(setup_copied, n - 7)
                rows, cols = src.shape[0], src.shape[1]
                nc.tensor.transpose(bank(n % 8)[0:cols, 0:rows], src, ident[0:rows, 0:rows]).then_inc(setup_turned, 1)
            pe.wait_ge(setup_copied, len(turns))
            for c in range(2):
                nc.tensor.matmul(bank(S0)[:, 0:QK], cwT_slots[:, c], qkv1T[:, c, 0:QK], start=c == 0, stop=c == 1)
            for c in range(2):
                nc.tensor.matmul(bank(S0 + 1)[:, 0:EMBED], cwT_slots[:, c], qkv1T[:, c, QK:], start=c == 0, stop=c == 1)
            nc.tensor.matmul(bank(S0 + 2)[:, 0:EMBED], cw_slots[:], cw_row[:], start=True, stop=True
                             ).then_inc(rep_done, 1)
            pe.wait_ge(w_one_ready, 1)
            pe.wait_ge(zeroed, 1)
            pe.wait_ge(masks_ready, 2)
            pe.wait_ge(nat_loaded[8], 64)

            t_banks, s_pairs, a_banks = ([Bank(), Bank()] for _ in range(3))

            def turn_pair(k, i, b, u):
                if u == 0:
                    pe.wait_ge(split_ready[k], b + 1)
                    pe.wait_ge(lo_ready[k], 2 * b + 2)
                t_banks[u % 2].take(pe, i, [head_copy(k, u)])
                to = bank(T0 + u % 2).bitcast(BF16)
                for h in range(2):
                    for a in range(2):
                        for s in range(2):
                            at = (2 * h + a) * TOK + s * HALF
                            mm = nc.tensor.transpose(to[:, at:at + HALF], split[k][:, 1 - a, s, 2 * u + h, :],
                                                     ident16[0:HALF, 0:HALF])
                mm.then_inc(turned[k], 1)

            def head_copy(k, u):
                act_copies = u in ACT_COPIES
                same = [v for v in range(u + 1) if (v in ACT_COPIES) == act_copies]
                per = len(ACT_COPIES) if act_copies else PAIRS - len(ACT_COPIES)
                return (heads_act if act_copies else heads_vec)[k], per, len(same), (2, 4)[k]

            def heads_copied(k, b):
                n = len(ACT_COPIES)
                pe.wait_ge(heads_act[k], n * b + n)
                pe.wait_ge(heads_vec[k], (PAIRS - n) * (b + 1))

            def pair_scores(k, i, p, lhs, done, read, stage):
                s_pairs[p % 2].take(pe, i, [(read, PAIRS, p + 1, stage)])
                for h in range(2):
                    for s in range(2):
                        hd = heads[k][:, 2 * p + h]
                        mm = nc.tensor.matmul(bank(S0 + 2 * (p % 2) + h)[0:HALF, s * TOK:s * TOK + TOK],
                                              hd[:, lhs, s * HALF:s * HALF + HALF], hd[:, 1 - lhs, :],
                                              start=True, stop=True)
                mm.then_inc(done, 1)

            def gather(k, i, b, g):
                if g == 0:
                    a_banks[0].take(pe, i, [(attended_ready[k], 2, 1, (2, 5)[k])])
                if g == 2:
                    a_banks[1].take(pe, i, [(attended_ready[k], 2, 2, (2, 5)[k])])
                pe.wait_ge(exped[k], PAIRS * b + 2 * g + 2)
                to = bank(A0)[:, g * TOK:g * TOK + TOK] if g < 2 else bank(A1)[:, 0:TOK]
                for s in range(2):
                    for h in range(4):
                        mm = nc.tensor.matmul(to[32 * h:32 * h + 32], values[k][:, s, 4 * g + h, :],
                                              probs[k][:, g % 2, h, s * TOK:s * TOK + TOK],
                                              start=s == 0, stop=s == 1, skip_group_check=True)
                mm.then_inc(gathered[k], 1)

            def steps(name, i, b):
                k = int(name[0]) // 3
                part = name[1]
                n = int(name[2]) if len(name) > 2 else 0
                if name == "0p":
                    pe.wait_ge(rows_summed, b + 1)
                    t_banks[1].take(pe, i, [(pooled_split, 1, 1, 0)])
                    for c in range(2):
                        mm = nc.tensor.matmul(bank(T1)[:, 0:TOK], pool_sel[:, c], row_sums[:, c],
                                              start=c == 0, stop=c == 1)
                    mm.then_inc(pooled_raw, 1)
                if part == "p" and name != "0p":
                    pe.wait_ge(pooled_split, b + 1)
                    s_pairs[n].take(pe, i, [(read, 2, n + 1, 1) for read in (qk1_copied, squared, hv_copied)])
                    lhs = pooled[:, HALF * n:HALF * n + HALF]
                    nc.tensor.matmul(bank(S0 + 2 * n)[0:HALF, 0:QK], lhs, w_one[:, 0:QK], start=True, stop=True)
                    nc.tensor.matmul(bank(S0 + 2 * n + 1)[0:HALF, 0:QK], lhs, w_one[:, QK:],
                                     start=True, stop=True).then_inc(first_proj, 1)
                if name == "3x":
                    pe.wait_ge(x2_ready, 2 * b + 2)
                    t_banks[0].take(pe, i, [(x2T_ready, 1, 1, 3)])
                    for c in range(2):
                        for s in range(2):
                            mm = nc.tensor.transpose(bank(T0)[0:96, c * TOK + s * HALF:c * TOK + s * HALF + HALF],
                                                     x2[:, s, 96 * c:96 * c + 96], ident[0:HALF, 0:HALF])
                    mm.then_inc(x2_turned, 1)
                if name == "3g":
                    pe.wait_ge(x2T_ready, b + 1)
                    t_banks[1].take(pe, i, [(down_ready, 1, 1, 3)])
                    width = W2_COLS - W2_LORA
                    for s in range(2):
                        for c in range(2):
                            mm = nc.tensor.matmul(bank(T1)[0:HALF, s * width:s * width + width],
                                                  x2T[0:96 + c, c, s * HALF:s * HALF + HALF],
                                                  w_two[0:96 + c, c, W2_LORA:], start=c == 0, stop=c == 1)
                    mm.then_inc(gated, 1)
                if name == "3d":
                    pe.wait_ge(down_ready, b + 1)
                    t_banks[0].take(pe, i, [(downT_ready, 1, 1, 3)])
                    for s in range(2):
                        mm = nc.tensor.transpose(bank(T0)[:, s * HALF:s * HALF + HALF], down[:, s], ident[0:HALF, 0:HALF])
                    mm.then_inc(down_turned, 1)
                if part in ("q", "v"):
                    if part == "q":
                        s_pairs[n].take(pe, i, [(read, 2, n + 1, 3) for read in (qk2_copied, v_copied)])
                    at = slice(n * HALF, n * HALF + HALF)
                    lo, hi, to, done = {"q": (0, W2_V, bank(S0 + 2 * n), second_qk_done),
                                        "v": (W2_V, W2_LORA, bank(S0 + 2 * n + 1), second_v_done)}[part]
                    to = to[0:HALF, 0:hi - lo]
                    for c in range(2):
                        nc.tensor.matmul(to, x2T[0:96 + c, c, at], w_two[0:96 + c, c, lo:hi], start=c == 0, stop=False)
                    if name == "3q0":
                        pe.wait_ge(downT_ready, b + 1)
                    nc.tensor.matmul(to, downT[:, at], w_lora[:, lo:hi], start=False, stop=True).then_inc(done, 1)
                if part == "t":
                    turn_pair(k, i, b, n)
                if name in ("4b0", "2a0"):
                    heads_copied(k, b)
                if part == "b":
                    pair_scores(1, i, n, 1, max_scored, max_taken, 4)
                if part == "a":
                    if k == 1 and n == 0:
                        pe.wait_ge(max_placed, QUADS * b + QUADS)
                    pair_scores(k, i, n, 0, scored[k], exped[k], int(name[0]))
                if part == "e":
                    if n == 0:
                        pe.wait_ge((values1_ready, values2_ready)[k], b + 1)
                    gather(k, i, b, n)
                if name in ("2g", "5g"):
                    gather(k, i, b, QUADS - 1)
                if part == "u":
                    if n == 0:
                        pe.wait_ge(max_parts_ready, b + 1)
                    t_banks[n % 2].take(pe, i, [(max_placed, QUADS, n + 1, 4)])
                    to = bank(T0 + n % 2).bitcast(BF16)
                    for h in range(4):
                        for s in range(2):
                            at = h * TOK + s * HALF
                            mm = nc.tensor.transpose(to[96:128, at:at + HALF], max_parts[:, s, 4 * n + h, :],
                                                     ident16[0:HALF, 0:HALF])
                    mm.then_inc(max_turned, 1)
                if part == "n":
                    pe.wait_ge(attended_ready[k], 2 * b + 2)
                    for s in range(2):
                        t_banks[s].take(pe, i, [(normed_ready[k], 1, 1, (2, 5)[k])])
                        for g in range(QUADS):
                            mm = nc.tensor.transpose(bank(T0 + s)[0:HALF, 128 * g:128 * g + 128],
                                                     attended[k][:, g, s * HALF:s * HALF + HALF], ident[:])
                    mm.then_inc(attended_turned[k], 1)
                if part == "m":
                    pe.wait_ge(normed_ready[k], b + 1)
                    t_banks[0].take(pe, i, [(normedT_ready[k], 1, 1, (2, 5)[k])])
                    for c in range(2):
                        for s in range(2):
                            mm = nc.tensor.transpose(bank(T0)[0:96, c * TOK + s * HALF:c * TOK + s * HALF + HALF],
                                                     normed[k][:, s, 96 * c:96 * c + 96], ident[0:HALF, 0:HALF])
                    mm.then_inc(normed_turned[k], 1)
                if part == "o":
                    pe.wait_ge(normedT_ready[k], b + 1)
                    a_banks[0].take(pe, i, [((h2_ready, result_ready)[k], 1, 1, (2, 5)[k])])
                    for s in range(2):
                        for c in range(2):
                            mm = nc.tensor.matmul(bank(A0)[0:HALF, s * EMBED:s * EMBED + EMBED],
                                                  normedT[k][:, c, s * HALF:s * HALF + HALF], w_proj[k][:, c],
                                                  start=c == 0, stop=c == 1)
                    mm.then_inc(projected[k], 1)

            steps("0p", -1, 0)
            iterations(pe, "pe", steps, t_banks + s_pairs + a_banks)

        @block.vector
        def _(dve):
            def fill(ap, value):
                nc.vector.memset(ap, value).then_inc(setup_vec, 1)
                fills[0] += 1

            fills = [0]
            for ap in (cw_slots[:], cwT_slots[:], pool_sel[:], w_two[:], values[0][:],
                       values[1][:], split[0][:], split[1][:], probs[1][:], max_parts[:], x2T[:], nothing[:]):
                fill(ap, 0.0)
            dve.wait_ge(setup_vec, fills[0])
            dve.wait_ge(pool_filled, 1)
            for k in range(2):
                fill(values[k][0:HALF, :, :, HD:HD + 1], 1.0)
            fill(split[1][:, 1, :, :, 6 * HD:6 * HD + 3], 1.0)
            fill(x2T[96:97, 1, :], 1.0)
            dve.wait_ge(setup_vec, fills[0])
            dve.wait_ge(ident_ready, 1)
            nc.vector.tensor_copy(ident16[:], ident[:]).then_inc(zeroed, 1)
            dve.wait_ge(masks_ready, 2)
            n = fills[0]
            for r, _ in POOL_SLOTS:
                nc.vector.tensor_copy(pool_sel[:, :, r:r + CHAN], pool_one[:])
                nc.vector.tensor_copy(cw_slots[:, r:r + CHAN], ident[0:CHAN, 0:CHAN])
            for part in range(3):
                spans = [ident[:, r:r + CHAN] for r, p in POOL_SLOTS if p == part]
                for m, span in enumerate(spans):
                    nc.vector.tensor_reduce(w_mean[:, 3 * part + m:3 * part + m + 1], span, X, ALU.add).then_inc(setup_vec, 1)
                    n += 1
            dve.wait_ge(setup_vec, n)
            for part in range(3):
                count = sum(p == part for _, p in POOL_SLOTS)
                nc.vector.tensor_reduce(part_mask[:, part:part + 1], w_mean[:, 3 * part:3 * part + count], X, ALU.add
                                        ).then_inc(setup_vec, 1)
                n += 1
            dve.wait_ge(nat_loaded[0], 16)
            nc.vector.tensor_reduce(cw_mean[:], cw_row[:], X, ALU.add).then_inc(setup_vec, 1)
            n += 1
            dve.wait_ge(setup_vec, n)
            nc.vector.tensor_scalar(cw_mean[:], cw_mean[:], 1.0 / EMBED, None, ALU.mult).then_inc(setup_vec, 1)
            n += 1
            dve.wait_ge(setup_vec, n)
            nc.vector.tensor_scalar(cw_mid[:], cw_row[:], cw_mean[:, 0:1], None, ALU.subtract).then_inc(cw_centred, 1)
            for m, (_, _, src, dsts) in enumerate(turns):
                dve.wait_ge(setup_turned, m + 1)
                rows, cols = src.shape[0], src.shape[1]
                for dst in dsts:
                    ins = nc.vector.tensor_copy(dst, bank(m % 8)[0:cols, 0:rows])
                ins.then_inc(setup_copied, 1)
            dve.wait_ge(rep_done, 1)
            for lo, b in ((0, S0), (QK, S0 + 2), (QK + EMBED, S0 + 1)):
                width = QK if lo == 0 else EMBED
                nc.vector.tensor_copy(w_rep[:, lo:lo + width], bank(b)[:, 0:width]).then_inc(setup_vec, 1)
                n += 1
            dve.wait_ge(setup_vec, n)
            qk_heads = w_rep[:, 0:QK].rearrange("p (h d) -> p h d", d=HD)
            nc.vector.tensor_reduce(w_mean[:], qk_heads, X, ALU.add).then_inc(setup_vec, 1)
            n += 1
            dve.wait_ge(setup_vec, n)
            nc.vector.tensor_scalar(w_mean[:], w_mean[:], 1.0 / HD, None, ALU.mult).then_inc(setup_vec, 1)
            n += 1
            dve.wait_ge(setup_vec, n)
            for step in (
                lambda: nc.vector.tensor_tensor(qk_heads, qk_heads,
                                                w_mean[:].unsqueeze(2).to_broadcast([128, 2 * HEADS, HD]), ALU.subtract),
                lambda: nc.vector.tensor_scalar(qk_heads, qk_heads, EPS ** -0.5, None, ALU.mult),
                lambda: nc.vector.tensor_copy(w_hi[:], w_rep[:]),
                lambda: nc.vector.tensor_tensor(w_rest[:], w_rep[:], w_hi[:], ALU.subtract),
                lambda: nc.vector.tensor_scalar(w_one[:], w_hi[:], part_mask[:, 0:1], None, ALU.mult),
                lambda: nc.vector.tensor_copy(w_hi[:], w_rest[:]),
                lambda: nc.vector.tensor_tensor(w_lo[:], w_rest[:], w_hi[:], ALU.subtract),
                lambda: nc.vector.scalar_tensor_tensor(out=w_one[:], in0=w_hi[:], scalar=part_mask[:, 1:2],
                                                       in1=w_one[:], op0=ALU.mult, op1=ALU.add),
            ):
                step().then_inc(setup_vec, 1)
                n += 1
                dve.wait_ge(setup_vec, n)
            nc.vector.scalar_tensor_tensor(out=w_one[:], in0=w_lo[:], scalar=part_mask[:, 2:3], in1=w_one[:],
                                           op0=ALU.mult, op1=ALU.add).then_inc(w_one_ready, 1)

            def sum_rows(b):
                dve.wait_ge(x_quartered, b + 1)
                dve.wait_ge(pooled_raw, b)
                nc.vector.tensor_reduce(row_sums[:].rearrange("p c t -> p (c t)"), x_quarter[:], X, ALU.add
                                        ).then_inc(rows_summed, 1)

            def split_pooled(b):
                dve.wait_ge(pooled_raw, b + 1)
                pool_steps.start(b)
                raw = bank(T1)[:, 0:TOK]
                pool_steps.link(dve, nc.vector.tensor_copy(pooled[:], raw))
                pool_steps.link(dve, nc.vector.tensor_tensor(pooled_rest[:], raw, pooled[:], ALU.subtract))
                pool_steps.link(dve, nc.vector.tensor_copy(pooled[64:128], pooled_rest[64:128]))
                nc.vector.tensor_tensor(pooled[96:128], pooled_rest[96:128], pooled[96:128], ALU.subtract
                                        ).then_inc(pooled_split, 1)

            def split_qk(k, b):
                dve.wait_ge(hi_ready[k], b + 1)
                dve.wait_ge(lo_ready[k], 2 * b)
                slots, _, _, flat, rest = slots_of(k)
                nc.vector.tensor_tensor(rest, flat, slots[:, :, 0], ALU.subtract).then_inc(rest_ready[k], 1)
                dve.wait_ge(rest_ready[k], b + 1)
                nc.vector.tensor_copy(slots[:, :, 1], rest).then_inc(mid_ready[k], 1)

            def repeat_parts(k, b):
                dve.wait_ge(mid_ready[k], b + 1)
                slots, q, kk, _, _ = slots_of(k)
                for at, part in ((3, 0), (4, 1), (5, 0)):
                    nc.vector.tensor_copy(slots[:, q, at], slots[:, q, part])
                for at, part in ((2, 0), (3, 1), (4, 0)):
                    ins = nc.vector.tensor_copy(slots[:, kk, at], slots[:, kk, part])
                ins.then_inc(split_ready[k], 1)

            def copy_heads(k, b, u):
                dve.wait_ge(turned[k], PAIRS * b + u + 1)
                heads_free(dve, k, b, u)
                nc.vector.tensor_copy(heads[k][:, 2 * u:2 * u + 2].rearrange("p h a t -> p (h a t)"),
                                      bank(T0 + u % 2).bitcast(BF16)[:, 0:4 * TOK]).then_inc(heads_vec[k], 1)

            def normalise(k, b, steps):
                dve.wait_ge(attended_turned[k], b + 1)
                src = bank(T0, 2)[0:HALF].rearrange("p (s c) -> p s c", s=2)[:, :, 0:32 * HEADS].rearrange(
                    "p s (h r) -> p s h r", r=32)
                steps.link(dve, nc.vector.reciprocal(den_inv[k][:], src[:, :, :, HD]))
                nc.vector.tensor_tensor(normed[k][:].rearrange("p s (h d) -> p s h d", d=HD), src[:, :, :, 0:HD],
                                        den_inv[k][:].unsqueeze(3).to_broadcast([HALF, 2, HEADS, HD]), ALU.mult
                                        ).then_inc(normed_ready[k], 1)

            def rsqrt(steps, y, x, tmp):
                steps.link(dve, nc.vector.tensor_scalar(y.bitcast(I32), x.bitcast(I32), -0.5, float(RSQRT_GUESS),
                                                        ALU.mult, ALU.add))
                for n in range(3):
                    steps.link(dve, nc.vector.tensor_tensor(tmp, y, y, ALU.mult))
                    steps.link(dve, nc.vector.scalar_tensor_tensor(out=tmp, in0=tmp, scalar=-0.5, in1=x,
                                                                   op0=ALU.mult, op1=ALU.mult))
                    ins = nc.vector.scalar_tensor_tensor(out=y, in0=tmp, scalar=1.5, in1=y,
                                                         op0=ALU.add, op1=ALU.mult)
                    if n < 2:
                        steps.link(dve, ins)
                return ins

            def norm_sums(i, first, second):
                links = norm_steps if first else last_norm_steps
                links.start(i if first else i - BATCH)
                if first:
                    dve.wait_ge(squared, 2 * i + 2)
                    nc.vector.tensor_reduce(sq_sum[:], qk_sq[:].rearrange("p a s (h d) -> p (a s h) d", d=HD), X, ALU.add)
                    dve.wait_ge(hv_copied, 2 * i + 2)
                    for s in range(2):
                        ins = nc.vector.bn_stats(bn6[:, s], hv[:, s, 0:EMBED])
                if second:
                    dve.wait_ge(h2_ready, i - 1)
                    for s in range(2):
                        ins = nc.vector.bn_stats(bn6[:, 2 + s], h2[:, s])
                links.link(dve, ins)

            def norm_factors(i, first, second):
                links = norm_steps if first else last_norm_steps
                w = slice(0 if first else 2, 4 if second else 2)
                bn, variances = bn6[:, w], var1[:, LN1 + w.start:LN1 + w.stop]
                nc.vector.tensor_tensor(gap[:, 0, w], bn[:, :, 1], bn[:, :, 4], ALU.subtract)
                links.link(dve, nc.vector.scalar_tensor_tensor(
                    out=gap[:, 2, w], in0=bn[:, :, 2], scalar=EMBED * EPS, in1=bn[:, :, 5], op0=ALU.add, op1=ALU.add))
                links.link(dve, nc.vector.scalar_tensor_tensor(
                    out=gap[:, 1, w], in0=gap[:, 0, w], scalar=0.25, in1=gap[:, 0, w], op0=ALU.mult, op1=ALU.mult))
                links.link(dve, nc.vector.scalar_tensor_tensor(
                    out=variances, in0=gap[:, 2, w], scalar=1.0 / EMBED, in1=gap[:, 1, w], op0=ALU.mult, op1=ALU.add))
                if second:
                    nc.vector.scalar_tensor_tensor(out=mean2[:], in0=gap[:, 0, 2:4], scalar=-0.5, in1=bn6[:, 2:4, 1],
                                                   op0=ALU.mult, op1=ALU.add)
                if first:
                    sums = sq_sum[:].rearrange("p (a s h) -> p a s h", a=2, s=2)
                    to = var1[:, 0:LN1].rearrange("p (a s h) -> p a s h", a=2, s=2)
                    for s in range(2):
                        ins = nc.vector.tensor_scalar(to[:, :, s], sums[:, :, s], 1.0 / HD, var1[:, LN1 + s:LN1 + s + 1],
                                                      ALU.mult, ALU.add)
                    links.link(dve, ins)
                    dve.wait_ge(values1_ready, i)
                    dve.wait_ge(scaled, i)
                at = slice(0 if first else LN2, LN2 + 2 if second else LN2)
                rsqrt(links, rs1[:, at], var1[:, at], nt1[:, at]).then_inc(rs1_ready, 1)
                links.end()

            sum_rows(0)
            split_pooled(0)

            def steps(name, i, b):
                k = int(name[0]) // 3
                part = name[1]
                n = int(name[2]) if len(name) > 2 else 0
                if name == "0q":
                    sum_rows(b)
                if name == "0p":
                    split_pooled(b)
                if name in ("1s", "1f"):
                    second = not (isinstance(i, int) and i < 2)
                    (norm_sums if name == "1s" else norm_factors)(i, True, second)
                if part == "w":
                    split_qk(k, b)
                if part == "z":
                    repeat_parts(k, b)
                if part == "t" and n not in ACT_COPIES:
                    copy_heads(k, b, n)
                if name == "2n":
                    two_steps.start(b)
                    normalise(0, b, two_steps)
                    two_steps.end()
                if name == "2o":
                    dve.wait_ge(projected[0], b + 1)
                    dve.wait_ge(h_kept_ready, b + 1)
                    dve.wait_ge(residual2_ready, b)
                    dve.wait_ge(x2_ready, 2 * b)
                    nc.vector.tensor_tensor(h2[:], bank(A0)[0:HALF, 0:2 * EMBED].rearrange("p (s e) -> p s e", s=2),
                                            h_kept[:], ALU.add).then_inc(h2_ready, 1)
                if name == "3l":
                    if isinstance(i, int) and i >= BATCH:
                        norm_sums(i, False, True)
                        norm_factors(i, False, True)
                    dve.wait_ge(rs1_ready, i + 1)
                    dve.wait_ge(x2_turned, b)
                    for s in range(2):
                        nc.vector.tensor_scalar(x2[:, s], h2[:, s], mean2[:, s:s + 1], rs1[:, LN2 + s:LN2 + s + 1],
                                                ALU.subtract, ALU.mult).then_inc(x2_ready, 1)
                if name == "3g":
                    three_steps.start(b)
                    dve.wait_ge(gated, b + 1)
                    both = bank(T1)[0:HALF, 0:2 * (W2_COLS - W2_LORA)].rearrange("p (s c) -> p s c", s=2)
                    nc.vector.tensor_copy(logits[:], both[:, :, LORA:])
                    three_steps.link(dve, nc.vector.tensor_reduce(lmax[:], both[:, :, LORA:], X, ALU.max))
                    nc.vector.tensor_tensor(shifted[:], logits[:], lmax[:].unsqueeze(2).to_broadcast([HALF, 2, EXPERTS]),
                                            ALU.subtract).then_inc(shifted_ready, 1)
                    full = [HALF, 2, EXPERTS, EXPERTS]
                    lj, li = logits[:].unsqueeze(2).to_broadcast(full), logits[:].unsqueeze(3).to_broadcast(full)
                    nc.vector.tensor_tensor(beats[:, :, :, 0:EXPERTS], lj, li, ALU.is_gt)
                    three_steps.link(dve, nc.vector.tensor_tensor(ties[:], lj, li, ALU.is_equal))
                    nc.vector.tensor_tensor(beats[:, :, :, EXPERTS:], ties[:], lower[:].unsqueeze(1).to_broadcast(full),
                                            ALU.mult)
                    dve.wait_ge(gexp_ready, b + 1)
                    three_steps.link(dve, nc.vector.tensor_reduce(gsum[:], gexp[:], X, ALU.add))
                    nc.vector.tensor_reduce(rank[:], beats[:], X, ALU.add)
                    three_steps.link(dve, nc.vector.reciprocal(ginv[:], gsum[:]))
                    three_steps.link(dve, nc.vector.scalar_tensor_tensor(
                        out=dispatch[:], in0=rank[:], scalar=1.5, in1=gexp[:], op0=ALU.is_lt, op1=ALU.mult))
                    three_steps.link(dve, nc.vector.scalar_tensor_tensor(
                        out=dispatch[:], in0=dispatch[:], scalar=LORA_SCALE,
                        in1=ginv[:].unsqueeze(2).to_broadcast([HALF, 2, EXPERTS]), op0=ALU.mult, op1=ALU.mult))
                    nc.vector.tensor_tensor(
                        down[:].rearrange("p s (n r) -> p s n r", r=RANK),
                        both[:, :, 0:LORA].rearrange("p s (n r) -> p s n r", r=RANK),
                        dispatch[:].unsqueeze(3).to_broadcast([HALF, 2, EXPERTS, RANK]), ALU.mult).then_inc(down_ready, 1)
                    three_steps.end()
                if part == "b":
                    dve.wait_ge(max_scored, PAIRS * b + n + 1)
                    src = bank(S0 + 2 * (n % 2), 2)[0:HALF].rearrange("p (n c) -> p n c", n=2)[:, :, 0:2 * TOK]
                    nc.vector.tensor_reduce(smax[:, 2 * n:2 * n + 2], src.rearrange("p n (s t) -> p n s t", s=2),
                                            X, ALU.max).then_inc(max_taken, 1)
                if part == "k":
                    four_steps.start(b)
                    dve.wait_ge(max_taken, PAIRS * b + PAIRS)
                    mx = smax[:].rearrange("p h s -> p s h")
                    four_steps.link(dve, nc.vector.tensor_scalar(max_parts[:, :, :, 0], mx, -1.0, None, ALU.mult))
                    four_steps.link(dve, nc.vector.scalar_tensor_tensor(
                        out=smax_rest[:], in0=mx, scalar=-1.0, in1=max_parts[:, :, :, 0], op0=ALU.mult, op1=ALU.subtract))
                    four_steps.link(dve, nc.vector.tensor_copy(max_parts[:, :, :, 1], smax_rest[:]))
                    nc.vector.tensor_tensor(max_parts[:, :, :, 2], smax_rest[:], max_parts[:, :, :, 1], ALU.subtract
                                            ).then_inc(max_parts_ready, 1)
                    four_steps.end()
                if name == "5n":
                    five_steps.start(b)
                    normalise(1, b, five_steps)
                    five_steps.end()
                if name == "5o":
                    dve.wait_ge(projected[1], b + 1)
                    dve.wait_ge(residual_ready, b + 1)
                    dve.wait_ge(stored, 16 * b)
                    nc.vector.tensor_tensor(result[:], bank(A0)[0:HALF, 0:2 * EMBED].rearrange("p (s e) -> p s e", s=2),
                                            residual[:], ALU.add).then_inc(result_ready, 1)

            iterations(dve, "vec", steps)


_INS = ["x", "L0_tok_channel_weights", "L0_attn_qkv_weight", "L0_attn_proj_weight", "L0_ffn_W_qkv", "L0_ffn_b_qkv",
        "L0_ffn_W_gate", "L0_ffn_b_gate", "L0_ffn_A", "L0_ffn_B_lora", "L0_ffn_W_proj", "L0_ffn_b_proj"]
_OUTS = [((BATCH, TOK, EMBED), "float32")]


def kernel(**inputs):
    import numpy as _np
    import concourse.bacc as _bacc
    from concourse import mybir as _mybir
    from concourse.bass_utils import run_bass_kernel_spmd as _run

    nc = _bacc.Bacc("TRN2", target_bir_lowering=False, num_devices=1)
    arrays, args = {}, []
    for name in _INS:
        a = _np.ascontiguousarray(inputs[name])
        arrays[f"in_{name}_dram"] = a
        args.append(nc.dram_tensor(f"in_{name}_dram", a.shape, _mybir.dt.from_np(a.dtype), kind="ExternalInput").ap())
    for i, (shape, dtype) in enumerate(_OUTS):
        dt = _mybir.dt.from_np(_np.dtype(dtype))
        args.append(nc.dram_tensor(f"out_{i}_dram", shape, dt, kind="ExternalOutput").ap())
    build(nc, *args)
    r = _run(nc, [arrays], core_ids=[0])
    return r.results[0]["out_0_dram"]
```
